# Optimizing a Trainium2 kernel written in Bass

```python
import numpy as np
import jax
import jax.numpy as jnp

def _softmax(x, axis=-1):
    return jax.nn.softmax(x, axis=axis)

def _gelu(x):
    return jax.nn.gelu(x, approximate=True)

def _silu(x):
    return jax.nn.silu(x)

def _sigmoid(x):
    return jax.nn.sigmoid(x)

def _layernorm(x, axis=-1, eps=1e-05):
    m = jnp.mean(x, axis=axis, keepdims=True)
    v = jnp.var(x, axis=axis, keepdims=True)
    return (x - m) / jnp.sqrt(v + eps)

def _scatter_add(tgt, idx, src, axis=0):
    return tgt.at[idx].add(src)

def _segment_sum(src, seg, n):
    return jax.ops.segment_sum(src, seg, n)
kernel_name = 'mk_metaformer_d2_conv_nhwc512_r4_d81c88'

def setup_inputs(seed: int=0):
    np.random.seed(seed)
    _w = jnp.asarray

    def _rec_inputs():
        import jax
        import jax.numpy as jnp
        _gk = jax.random.key(seed)
        x = -0.000125 + 0.9999 * jax.random.normal(jax.random.fold_in(_gk, 1), (4, 32, 32, 128), jnp.float32)
        return x
    x = _rec_inputs()

    def _L0_conv_setup():
        import jax, jax.numpy as jnp
        import numpy as np
        DIM = 128
        HEADS = 16
        HD = DIM // HEADS
        WH, WW = (8, 8)
        D0, D1 = (2, 2)
        TWH, TWW = (WH * D0, WW * D1)
        SCALE = HD ** (-0.5)

        def _wpart(x, wh, ww):
            B, H, W, C = x.shape
            x = x.reshape(B, H // wh, wh, W // ww, ww, C)
            return x.transpose(0, 1, 3, 2, 4, 5).reshape(-1, wh, ww, C)

        def _wrev(win, wh, ww, H, W):
            C = win.shape[-1]
            B = win.shape[0] // (H // wh * (W // ww))
            x = win.reshape(B, H // wh, W // ww, wh, ww, C).transpose(0, 1, 3, 2, 4, 5)
            return x.reshape(B, H, W, C)

        def _rope2(x):
            d = HD // 2
            inv = 1.0 / 10000.0 ** (jnp.arange(0, d, 2, dtype=jnp.float32) / d)

            def rot(xp, ang):
                x1, x2 = (xp[..., 0::2], xp[..., 1::2])
                c, s = (jnp.cos(ang), jnp.sin(ang))
                return jnp.stack([x1 * c - x2 * s, x1 * s + x2 * c], axis=-1).reshape(xp.shape)
            ah = (jnp.arange(WH, dtype=jnp.float32)[:, None] * inv)[:, None, :]
            aw = (jnp.arange(WW, dtype=jnp.float32)[:, None] * inv)[None, :, :]
            return jnp.concatenate([rot(x[..., :d], ah), rot(x[..., d:], aw)], axis=-1)

        def _forward(x, qkv_w, qkv_b, proj_w, proj_b):
            B, H, W, C = x.shape
            xw = _wpart(x, TWH, TWW)
            B_ = xw.shape[0]
            xw = _wpart(xw, D0, D1)
            xw = xw.reshape(B_, WH * WW, D0 * D1, C)
            xw = xw.transpose(0, 2, 1, 3).reshape(B_ * D0 * D1, WH * WW, C)
            B__, N = (xw.shape[0], xw.shape[1])
            qkv = (xw @ qkv_w.T + qkv_b).reshape(B__, N, 3, HEADS, HD).transpose(2, 0, 3, 1, 4)
            q, k, v = (qkv[0], qkv[1], qkv[2])
            q = _rope2(q.reshape(-1, WH, WW, HD)).reshape(B__, HEADS, N, HD) * SCALE
            k = _rope2(k.reshape(-1, WH, WW, HD)).reshape(B__, HEADS, N, HD)
            attn = jax.nn.softmax(jnp.einsum('bhnd,bhmd->bhnm', q, k), axis=-1)
            out = jnp.einsum('bhnm,bhmd->bhnd', attn, v)
            out = out.transpose(0, 2, 1, 3).reshape(B__, N, C)
            out = out.reshape(B_, D0 * D1, N, C).transpose(0, 2, 1, 3).reshape(-1, D0, D1, C)
            out = _wrev(out, D0, D1, TWH, TWW)
            out = _wrev(out, TWH, TWW, H, W)
            return out @ proj_w.T + proj_b
        key = jax.random.key(seed)
        k0, k1, k2 = jax.random.split(key, 3)
        x = jax.random.normal(k0, (4, 32, 32, DIM), dtype=jnp.float32)
        qkv_w = jax.random.normal(k1, (3 * DIM, DIM), dtype=jnp.float32) * DIM ** (-0.5)
        qkv_b = jnp.zeros((3 * DIM,), dtype=jnp.float32)
        proj_w = jax.random.normal(k2, (DIM, DIM), dtype=jnp.float32) * DIM ** (-0.5)
        proj_b = jnp.zeros((DIM,), dtype=jnp.float32)
        return {'x': x, 'qkv_w': qkv_w, 'qkv_b': qkv_b, 'proj_w': proj_w, 'proj_b': proj_b}
    _L0_conv_all = _L0_conv_setup()
    _L0_conv_in = {k: v for k, v in _L0_conv_all.items() if k in ('qkv_w', 'qkv_b', 'proj_w', 'proj_b')}
    del _L0_conv_all

    def _L0_ffn_setup():
        import jax, jax.numpy as jnp
        import numpy as np
        TOP_K = 2
        key = jax.random.key(seed)
        k0, k1, k2, k3, k4 = jax.random.split(key, 5)
        B, S, D, F, E = (1, 512, 128, 256, 8)
        scale = 0.02
        hidden_states = jax.random.normal(k0, (B, S, D), dtype=jnp.float32)
        router_w = jax.random.normal(k1, (D, E), dtype=jnp.float32) * scale
        w1 = jax.random.normal(k2, (E, D, F), dtype=jnp.float32) * scale
        w2 = jax.random.normal(k3, (E, F, D), dtype=jnp.float32) * scale
        w3 = jax.random.normal(k4, (E, D, F), dtype=jnp.float32) * scale
        return {'hidden_states': hidden_states, 'router_w': router_w, 'w1': w1, 'w2': w2, 'w3': w3}
    _L0_ffn_all = _L0_ffn_setup()
    _L0_ffn_in = {k: v for k, v in _L0_ffn_all.items() if k in ('router_w', 'w1', 'w2', 'w3')}
    del _L0_ffn_all

    def _L1_conv_setup():
        import jax, jax.numpy as jnp
        import numpy as np
        EPS = 1e-07
        ITERS = 3
        MEMBERS = 32
        key = jax.random.key(seed)
        k1, k2, k3 = jax.random.split(key, 3)
        B, H, W, C = (32, 48, 48, 128)
        x = jax.random.normal(k1, (B, H, W, C), dtype=jnp.float32)
        gamma = jax.random.uniform(k2, (1, 1, 1, C), dtype=jnp.float32)
        beta = jax.random.normal(k3, (1, 1, 1, C), dtype=jnp.float32)
        return {'x': x, 'gamma': gamma, 'beta': beta}
    _L1_conv_all = _L1_conv_setup()
    _L1_conv_in = {k: v for k, v in _L1_conv_all.items() if k in ('gamma', 'beta')}
    del _L1_conv_all

    def _L1_ffn_setup():
        import jax, jax.numpy as jnp
        import numpy as np
        B, S, D = (4, 512, 128)
        E, H, K = (8, 256, 2)

        def _moe_forward(x, router_w, router_b, w1, b1, wg, bg, wv, bv, w2, b2):
            b, s, d = x.shape
            xf = x.reshape(-1, d)
            T = xf.shape[0]
            scores = xf @ router_w + router_b
            probs = jax.nn.softmax(scores, axis=-1)
            topk_p, topk_i = jax.lax.top_k(probs, K)
            gates = jnp.zeros((T, E), xf.dtype).at[jnp.arange(T)[:, None], topk_i].set(topk_p)
            h = jnp.einsum('td,edh->teh', xf, w1) + b1[None]
            gated = jax.nn.silu(jnp.einsum('teh,ehf->tef', h, wg) + bg[None]) * (jnp.einsum('teh,ehf->tef', h, wv) + bv[None])
            y = jnp.einsum('tef,efd->ted', gated, w2) + b2[None]
            out = jnp.einsum('ted,te->td', y, gates)
            return out.reshape(b, s, d)
        key = jax.random.key(seed)
        ks = jax.random.split(key, 8)
        s_in = 0.02
        return {'x': jax.random.normal(ks[0], (B, S, D), jnp.float32), 'router_w': jax.random.normal(ks[1], (D, E), jnp.float32) * s_in, 'router_b': jnp.zeros((E,), jnp.float32), 'w1': jax.random.normal(ks[2], (E, D, H), jnp.float32) * s_in, 'b1': jnp.zeros((E, H), jnp.float32), 'wg': jax.random.normal(ks[3], (E, H, H), jnp.float32) * s_in, 'bg': jnp.zeros((E, H), jnp.float32), 'wv': jax.random.normal(ks[4], (E, H, H), jnp.float32) * s_in, 'bv': jnp.zeros((E, H), jnp.float32), 'w2': jax.random.normal(ks[5], (E, H, D), jnp.float32) * s_in, 'b2': jnp.zeros((E, D), jnp.float32)}
    _L1_ffn_all = _L1_ffn_setup()
    _L1_ffn_in = {k: v for k, v in _L1_ffn_all.items() if k in ('router_w', 'router_b', 'w1', 'b1', 'wg', 'bg', 'wv', 'bv', 'w2', 'b2')}
    del _L1_ffn_all
    return {'x': x, 'L0_conv_qkv_w': _L0_conv_in['qkv_w'], 'L0_conv_qkv_b': _L0_conv_in['qkv_b'], 'L0_conv_proj_w': _L0_conv_in['proj_w'], 'L0_conv_proj_b': _L0_conv_in['proj_b'], 'L0_ffn_router_w': _L0_ffn_in['router_w'], 'L0_ffn_w1': _L0_ffn_in['w1'], 'L0_ffn_w2': _L0_ffn_in['w2'], 'L0_ffn_w3': _L0_ffn_in['w3'], 'L1_conv_gamma': _L1_conv_in['gamma'], 'L1_conv_beta': _L1_conv_in['beta'], 'L1_ffn_router_w': _L1_ffn_in['router_w'], 'L1_ffn_router_b': _L1_ffn_in['router_b'], 'L1_ffn_w1': _L1_ffn_in['w1'], 'L1_ffn_b1': _L1_ffn_in['b1'], 'L1_ffn_wg': _L1_ffn_in['wg'], 'L1_ffn_bg': _L1_ffn_in['bg'], 'L1_ffn_wv': _L1_ffn_in['wv'], 'L1_ffn_bv': _L1_ffn_in['bv'], 'L1_ffn_w2': _L1_ffn_in['w2'], 'L1_ffn_b2': _L1_ffn_in['b2']}

def reference(x, L0_conv_qkv_w, L0_conv_qkv_b, L0_conv_proj_w, L0_conv_proj_b, L0_ffn_router_w, L0_ffn_w1, L0_ffn_w2, L0_ffn_w3, L1_conv_gamma, L1_conv_beta, L1_ffn_router_w, L1_ffn_router_b, L1_ffn_w1, L1_ffn_b1, L1_ffn_wg, L1_ffn_bg, L1_ffn_wv, L1_ffn_bv, L1_ffn_w2, L1_ffn_b2):
    import jax
    import jax.numpy as jnp

    def _L0_conv_ref(x, qkv_w, qkv_b, proj_w, proj_b):
        import jax, jax.numpy as jnp
        import numpy as np
        DIM = 128
        HEADS = 16
        HD = DIM // HEADS
        WH, WW = (8, 8)
        D0, D1 = (2, 2)
        TWH, TWW = (WH * D0, WW * D1)
        SCALE = HD ** (-0.5)

        def _wpart(x, wh, ww):
            B, H, W, C = x.shape
            x = x.reshape(B, H // wh, wh, W // ww, ww, C)
            return x.transpose(0, 1, 3, 2, 4, 5).reshape(-1, wh, ww, C)

        def _wrev(win, wh, ww, H, W):
            C = win.shape[-1]
            B = win.shape[0] // (H // wh * (W // ww))
            x = win.reshape(B, H // wh, W // ww, wh, ww, C).transpose(0, 1, 3, 2, 4, 5)
            return x.reshape(B, H, W, C)

        def _rope2(x):
            d = HD // 2
            inv = 1.0 / 10000.0 ** (jnp.arange(0, d, 2, dtype=jnp.float32) / d)

            def rot(xp, ang):
                x1, x2 = (xp[..., 0::2], xp[..., 1::2])
                c, s = (jnp.cos(ang), jnp.sin(ang))
                return jnp.stack([x1 * c - x2 * s, x1 * s + x2 * c], axis=-1).reshape(xp.shape)
            ah = (jnp.arange(WH, dtype=jnp.float32)[:, None] * inv)[:, None, :]
            aw = (jnp.arange(WW, dtype=jnp.float32)[:, None] * inv)[None, :, :]
            return jnp.concatenate([rot(x[..., :d], ah), rot(x[..., d:], aw)], axis=-1)

        def _forward(x, qkv_w, qkv_b, proj_w, proj_b):
            B, H, W, C = x.shape
            xw = _wpart(x, TWH, TWW)
            B_ = xw.shape[0]
            xw = _wpart(xw, D0, D1)
            xw = xw.reshape(B_, WH * WW, D0 * D1, C)
            xw = xw.transpose(0, 2, 1, 3).reshape(B_ * D0 * D1, WH * WW, C)
            B__, N = (xw.shape[0], xw.shape[1])
            qkv = (xw @ qkv_w.T + qkv_b).reshape(B__, N, 3, HEADS, HD).transpose(2, 0, 3, 1, 4)
            q, k, v = (qkv[0], qkv[1], qkv[2])
            q = _rope2(q.reshape(-1, WH, WW, HD)).reshape(B__, HEADS, N, HD) * SCALE
            k = _rope2(k.reshape(-1, WH, WW, HD)).reshape(B__, HEADS, N, HD)
            attn = jax.nn.softmax(jnp.einsum('bhnd,bhmd->bhnm', q, k), axis=-1)
            out = jnp.einsum('bhnm,bhmd->bhnd', attn, v)
            out = out.transpose(0, 2, 1, 3).reshape(B__, N, C)
            out = out.reshape(B_, D0 * D1, N, C).transpose(0, 2, 1, 3).reshape(-1, D0, D1, C)
            out = _wrev(out, D0, D1, TWH, TWW)
            out = _wrev(out, TWH, TWW, H, W)
            return out @ proj_w.T + proj_b
        return _forward(x, qkv_w, qkv_b, proj_w, proj_b)

    def _L0_ffn_ref(hidden_states, router_w, w1, w2, w3):
        import jax, jax.numpy as jnp
        import numpy as np
        TOP_K = 2
        B, S, D = hidden_states.shape
        E = router_w.shape[1]
        x = hidden_states.reshape(-1, D)
        T = x.shape[0]
        router_logits = x @ router_w
        probs = jax.nn.softmax(router_logits.astype(jnp.float32), axis=-1)
        routing_weights, selected_experts = jax.lax.top_k(probs, TOP_K)
        routing_weights = routing_weights / routing_weights.sum(axis=-1, keepdims=True)
        routing_weights = routing_weights.astype(x.dtype)
        combine = jnp.zeros((T, E), dtype=x.dtype).at[jnp.arange(T)[:, None], selected_experts].add(routing_weights)
        gate = jax.nn.silu(jnp.einsum('td,edf->tef', x, w1))
        up = jnp.einsum('td,edf->tef', x, w3)
        h = gate * up * combine[:, :, None]
        out = jnp.einsum('tef,efd->td', h, w2)
        return out.reshape(B, S, D)

    def _L1_conv_ref(x, gamma, beta):
        import jax, jax.numpy as jnp
        import numpy as np
        EPS = 1e-07
        ITERS = 3
        MEMBERS = 32
        B, H, W, C = x.shape
        m = MEMBERS
        g = C // m
        N = B * H * W
        f = jnp.transpose(x, (3, 0, 1, 2)).reshape(C, N)
        mean = jnp.mean(f, axis=1, keepdims=True)
        f = f - mean
        fg = f.reshape(g, m, N)
        cov = jnp.einsum('gmn,gkn->gmk', fg, fg) / (jnp.float32(N) - 1.0)
        eye = jnp.eye(m, dtype=jnp.float32)
        cov = (1.0 - EPS) * cov + EPS * eye[None]
        tr = jnp.einsum('gii->g', cov)[:, None, None]
        sig = cov / tr
        P = jnp.broadcast_to(eye, (g, m, m))
        for _ in range(ITERS):
            P = (3.0 * P - P @ P @ P @ sig) / 2.0
        whiten = P / jnp.sqrt(tr)
        fhat = jnp.einsum('gmk,gkn->gmn', whiten, fg)
        out = fhat.reshape(C, B, H, W).transpose(1, 2, 3, 0)
        return out * gamma + beta

    def _L1_ffn_ref(x, router_w, router_b, w1, b1, wg, bg, wv, bv, w2, b2):
        import jax, jax.numpy as jnp
        import numpy as np
        B, S, D = (4, 512, 128)
        E, H, K = (8, 256, 2)

        def _moe_forward(x, router_w, router_b, w1, b1, wg, bg, wv, bv, w2, b2):
            b, s, d = x.shape
            xf = x.reshape(-1, d)
            T = xf.shape[0]
            scores = xf @ router_w + router_b
            probs = jax.nn.softmax(scores, axis=-1)
            topk_p, topk_i = jax.lax.top_k(probs, K)
            gates = jnp.zeros((T, E), xf.dtype).at[jnp.arange(T)[:, None], topk_i].set(topk_p)
            h = jnp.einsum('td,edh->teh', xf, w1) + b1[None]
            gated = jax.nn.silu(jnp.einsum('teh,ehf->tef', h, wg) + bg[None]) * (jnp.einsum('teh,ehf->tef', h, wv) + bv[None])
            y = jnp.einsum('tef,efd->ted', gated, w2) + b2[None]
            out = jnp.einsum('ted,te->td', y, gates)
            return out.reshape(b, s, d)
        return _moe_forward(x, router_w, router_b, w1, b1, wg, bg, wv, bv, w2, b2)

    def _gn(v, G=32, eps=1e-05):
        B_, H_, W_, C_ = v.shape
        g = v.reshape(B_, H_, W_, G, C_ // G)
        m = jnp.mean(g, axis=(1, 2, 4), keepdims=True)
        s = jnp.var(g, axis=(1, 2, 4), keepdims=True)
        return ((g - m) / jnp.sqrt(s + eps)).reshape(v.shape)

    def _ln_c(v, eps=1e-06):
        m = jnp.mean(v, axis=-1, keepdims=True)
        s = jnp.var(v, axis=-1, keepdims=True)
        return (v - m) / jnp.sqrt(s + eps)

    def _ln_t(v, eps=1e-05):
        m = jnp.mean(v, axis=-1, keepdims=True)
        s = jnp.var(v, axis=-1, keepdims=True)
        return (v - m) / jnp.sqrt(s + eps)

    def _to_tokens(v):
        B_, H_, W_, C_ = v.shape
        return v.reshape(B_, H_ * W_, C_)

    def _from_tokens(t, like):
        return t.reshape(like.shape)
    x = x + _L0_conv_ref(_ln_c(x), L0_conv_qkv_w, L0_conv_qkv_b, L0_conv_proj_w, L0_conv_proj_b)
    t = _to_tokens(x)
    t = t + _L0_ffn_ref(_ln_t(t), L0_ffn_router_w, L0_ffn_w1, L0_ffn_w2, L0_ffn_w3)
    x = _from_tokens(t, x)
    x = x + _L1_conv_ref(_ln_c(x), L1_conv_gamma, L1_conv_beta)
    t = _to_tokens(x)
    t = t + _L1_ffn_ref(_ln_t(t), L1_ffn_router_w, L1_ffn_router_b, L1_ffn_w1, L1_ffn_b1, L1_ffn_wg, L1_ffn_bg, L1_ffn_wv, L1_ffn_bv, L1_ffn_w2, L1_ffn_b2)
    x = _from_tokens(t, x)
    return x

_drawn_inputs = setup_inputs


def setup_inputs(seed=0):
    import zlib

    import numpy as np

    out = dict(_drawn_inputs(seed))
    spreads = {'L0_conv_qkv_b': (0.0, 0.1),
     'L0_conv_proj_b': (0.0, 0.1),
     'L1_ffn_router_b': (0.0, 0.8),
     'L1_ffn_b1': (0.0, 0.8),
     'L1_ffn_bg': (0.0, 0.8),
     'L1_ffn_bv': (0.0, 0.8),
     'L1_ffn_b2': (0.0, 2.0)}
    factors = {'L0_ffn_router_w': 8.0,
     'L0_ffn_w1': 8.0,
     'L0_ffn_w2': 8.0,
     'L0_ffn_w3': 8.0,
     'L1_ffn_router_w': 4.379,
     'L1_ffn_w1': 8.0,
     'L1_ffn_wg': 8.0,
     'L1_ffn_wv': 8.0,
     'L1_ffn_w2': 8.0}
    for name, (base, spread) in spreads.items():
        noise = np.random.default_rng([zlib.crc32(name.encode()), seed]).standard_normal(out[name].shape)
        drawn = base * np.exp(spread * noise) if base else spread * noise
        out[name] = jnp.asarray(drawn.astype(out[name].dtype))
    for name, factor in factors.items():
        out[name] = (out[name] * factor).astype(out[name].dtype)
    return out
```

```python
import numpy as np
import concourse.bass as bass
from concourse import mybir
from contextlib import ExitStack

F32 = mybir.dt.float32
F32R = mybir.dt.float32r
BF16 = mybir.dt.bfloat16
ALU = mybir.AluOpType
ACT = mybir.ActivationFunctionType
AXIS_X = mybir.AxisListType.X

ONE = 1
P = 128
TOKENS = 4 * 32 * 32
TILES = TOKENS // P
BLOCK = 512
BLOCKS = TOKENS // BLOCK
BT = BLOCK // P
WIN = 64
BW = BLOCK // WIN
HEADS, HD = 16, 8
HP = HEADS // 2
E, FF = 8, 256
FT = FF // P
UNITS = E * FT
GROUPS, MEMBERS = 4, 32
SPLIT = 3
ATT_EPS, TOK_EPS, WHITEN_EPS = 1e-6, 1e-5, 1e-7
NEWTON_STEPS = 3


def constants():
    ch = np.arange(P)
    d = ch % HD
    head = ch // HD
    half = HD // 2
    inv = 1.0 / 10000.0 ** (2 * ((d % half) // 2) / half)
    n = np.arange(WIN)
    place = np.where(d[:, None] < half, n[None, :] // 8, n[None, :] % 8)
    ang = place * inv[:, None]
    cos, sin = np.cos(ang), np.sin(ang) * np.where(d % 2, 1.0, -1.0)[:, None]
    scale = HD ** -0.5
    e = np.arange(E)
    return {
        "ident": np.eye(P),
        "rope": np.concatenate([cos * scale, sin * scale, cos, sin], 1),
        "in_quad": (head[:, None] % 4 == np.arange(4)[None, :]),
        "earlier": np.broadcast_to((e[None, :] < e[:, None]).reshape(1, E * E), (P, E * E)),
        "mean": np.full((P, P), 1.0 / TOKENS),
        "same_group": (ch[:, None] // MEMBERS == ch[None, :] // MEMBERS),
        "minus_half": np.full((P, BT), -0.5),
    }


def half_constants():
    sel = np.zeros((P, E, P))
    for r in range(SPLIT * E):
        sel[r, r % E] = 1.0
    one = np.uint16(0x3F80)
    return np.concatenate([np.eye(P), sel.reshape(P, E * P)], 1).astype(np.uint16) * one


CONST_AT, CONST_WIDTH = {}, 0
for _name, _table in constants().items():
    CONST_AT[_name] = (CONST_WIDTH, _table.shape[1])
    CONST_WIDTH += _table.shape[1]

SMALL_AT, SMALL_WIDTH = {}, 0
for _name, _width in (("qk_bias", 4), ("v_bias", P), ("proj_bias", P), ("router0", E), ("router1", E),
                      ("router1_bias", E), ("gamma", P), ("beta", P), ("b1", UNITS), ("gv_bias", 2 * UNITS),
                      ("b2", P)):
    SMALL_AT[_name] = (SMALL_WIDTH, _width)
    SMALL_WIDTH += _width


def build(nc, x, const, halves, small, att_w, proj_w, w13, w2_0, w1gv, w2_1, out):
    ctx = ExitStack()
    with ctx:
        def sb(name, shape, dt=F32):
            return ctx.enter_context(nc.sbuf_tensor(name, shape, dt))

        def sem(name):
            return ctx.enter_context(nc.semaphore(name))

        counted = []

        def csem(name):
            counted.append(sem(name))
            return counted[-1]

        X = sb("X", [P, TILES, P])
        C = sb("C", [P, CONST_WIDTH])
        S = sb("S", [P, SMALL_WIDTH])
        qkv_w = sb("qkv_w", [P, 5, P])
        wo = sb("wo", [P, 5, P])
        half = sb("half", [P, P + E * P], mybir.dt.uint16)
        ident_b = half[:, 0:P].bitcast(BF16)
        select = half[0:SPLIT * E, P:P + E * P].bitcast(BF16).rearrange("r (e c) -> r e c", e=E)
        att_bias = sb("att_bias", [P, P])
        Wh = [sb(f"Wh{l}", [P, E, 2 * FF], F32R) for l in range(2)]
        Wl = [sb(f"Wl{l}", [P, E, 2 * FF], F32R) for l in range(2)]
        W2 = [sb(f"W2_{l}", [P, UNITS, P]) for l in range(2)]
        gv_bias = sb("gv_bias", [P, 2 * UNITS])
        region_a = sb("region_a", [P, 8 * BLOCK])
        Qm = region_a[:, 0:4 * BLOCK].rearrange("p (g t) -> p g t", g=4)
        Kbd = region_a[:, 4 * BLOCK:8 * BLOCK].rearrange("p (w j m) -> p w j m", w=BW, j=4)
        FT_ = region_a
        region_b = sb("region_b", [P, 8 * BLOCK])
        On = region_b[:, 0:4 * BLOCK].rearrange("p (j t) -> p j t", j=4)
        Sx = region_b[:, 4 * BLOCK:8 * BLOCK].rearrange("p (b s) -> p b s", b=2)
        Y2 = region_b[:, :].rearrange("p (t c) -> p t c", t=TILES)
        tq = sb("tq", [P, 2, BLOCK])
        tk = sb("tk", [P, 2, BLOCK])
        kr = tk[:, 0, :]
        PT = sb("PT", [P, HP, P])
        Vp = sb("Vp", [P, BW, HP * HD])
        ya = sb("ya", [P, BT, P])
        yaT = sb("yaT", [P, BLOCK])
        smax = sb("smax", [P, BT, HEADS])
        ssum = sb("ssum", [P, BT, HEADS])
        srec = sb("srec", [P, BT, HEADS])
        stats = {n: sb(f"stats_{n}", [P, BT, 6]) for n in "amc"}
        mv = {n: sb(f"mv_{n}", [P, BT, 2]) for n in "amc"}
        var = {n: sb(f"var_{n}", [P, BT]) for n in "amc"}
        rstd = {n: sb(f"rstd_{n}", [P, BT]) for n in "amc"}
        ym = sb("ym", [P, BT, P])
        ymT = sb("ymT", [P, BLOCK])
        xh = sb("xh", [P, BLOCK], F32R)
        xl = sb("xl", [P, BLOCK], F32R)
        lg = sb("lg", [P, BT, E])
        lmax = sb("lmax", [P, BT])
        lex = sb("lex", [P, BT, E])
        cmp1 = sb("cmp1", [P, BT, E, E])
        cmp2 = sb("cmp2", [P, BT, E, E])
        rank = sb("rank", [P, BT, E])
        gsum = sb("gsum", [P, BT])
        gate = sb("gate", [P, BT, E])
        gres = sb("gres", [P, BT, E])
        g3 = sb("g3", [P, BT, SPLIT, E], BF16)
        gT = sb("gT", [SPLIT * E, BLOCK], BF16)
        gTf = sb("gTf", [SPLIT * E, BLOCK])
        work = sb("work", [P, 8, BLOCK])
        csb, silu, h, h2 = (work[:, 2 * k:2 * k + 2, :] for k in range(4))
        raw0 = h2
        raw1 = work[:, 0:5, :].rearrange("p a n -> p (a n)").rearrange("p (s n) -> p s n", s=2)
        ob = sb("ob", [P, BLOCK])
        mean_c = sb("mean_c", [P, P])
        cov = sb("cov", [P, P])
        covd = sb("covd", [P, P])
        diag = sb("diag", [P, 1])
        trace = sb("trace", [P, 1])
        rtrace = sb("rtrace", [P, 1])
        rstrace = sb("rstrace", [P, 1])
        sig = sb("sig", [P, P])
        Pm = sb("Pm", [P, 2, P])
        N1 = sb("N1", [P, P])
        N2 = sb("N2", [P, P])
        tmpn = sb("tmpn", [P, P])
        whiten = sb("whiten", [P, P])
        fts = sb("fts", [P, BLOCK])

        def con(name):
            a, w = CONST_AT[name]
            return C[:, a:a + w]

        def par(name):
            a, w = SMALL_AT[name]
            return S[:, a:a + w]

        ident = con("ident")
        bank = ctx.enter_context(nc.psum_tensor("bank", [P, 8, 512], F32))
        C_BANK, ACC_BANK, ATT0, ATT1 = 4, 5, 6, 7

        def G(u):
            return bank[:, 2 * (u % 2), :]

        def U(u):
            return bank[:, 2 * (u % 2) + 1, :]

        ld_const, ld_small, ld_att, ld_x, ld_w13, ld_w2, ld_w1gv = (sem(f"ld_{n}") for n in (
            "const", "small", "att", "x", "w13", "w2", "w1gv"))
        w13_slot, w1gv_slot = [sem(f"w13_slot{k}") for k in range(2)], [sem(f"w1gv_slot{k}") for k in range(2)]
        setup = sem("setup")
        w0h, w0l = sem("w0h"), sem("w0l")
        fold_ps, w1h, w1l = sem("fold_ps"), sem("w1h"), sem("w1l")
        bias_ps, bias_sb = sem("bias_ps"), sem("bias_sb")
        abias_ps, abias_sb = sem("abias_ps"), sem("abias_sb")
        ln = {n: {k: csem(f"{k}_{n}") for k in ("stats", "mv", "var", "rstd", "y")} for n in "amc"}
        att_full, att_free = csem("att_full"), csem("att_free")
        yaT_sb, q_t, q_m, k_t, k_r, k_bd = (csem(n) for n in (
            "yaT_sb", "q_t", "q_m", "k_t", "k_r", "k_bd"))
        s_max, p_exp, p_sum, p_rec, p_nrm, x_att = (csem(n) for n in (
            "s_max", "p_exp", "p_sum", "p_rec", "p_nrm", "x_att"))
        prep_full, prep_free = csem("prep_full"), csem("prep_free")
        ymT_sb, xh_sb, xl_sb, l_lg, l_max, l_sub, l_exp, l_rank, l_sel, g_one, g_two, g_rec, g_sb, gT_sb, gTf_sb = (
            csem(n) for n in ("ymT_sb", "xh_sb", "xl_sb", "l_lg", "l_max", "l_sub", "l_exp", "l_rank", "l_sel",
                             "g_one", "g_two", "g_rec", "g_sb", "gT_sb", "gTf_sb"))
        c_full, c_free = csem("c_full"), csem("c_free")
        gu_full, g_free, u_free = csem("gu_full"), csem("g_free"), csem("u_free")
        h_sb, h2_sb, h2_used = csem("h_sb"), csem("h2_sb"), csem("h2_used")
        ob_sb, post_full, x_moe = csem("ob_sb"), csem("post_full"), csem("x_moe")
        mean_ps, mean_sb = sem("mean_ps"), sem("mean_sb")
        f_sb, cov_ps, ft_sb = (csem(n) for n in ("f_sb", "cov_ps", "ft_sb"))
        newton, newton_ps = sem("newton"), sem("newton_ps")
        wh_ready, fts_sb, wh_ps, x_wh = sem("wh_ready"), csem("fts_sb"), csem("wh_ps"), csem("x_wh")
        stored = sem("stored")
        wait_done = sem("wait_done")

        order = ["T", "Q", "K", "V", "S0", "S1", "T0", "O0", "S2", "T1", "O1", "S3", "T2", "O2", "T3", "O3", "J"]
        FILL = {name: k for k, name in enumerate(order)}
        FILLS = len(order)

        def xb(i):
            return X[:, bass.ds(i * BT, BT), :]

        def tile_of(t3, k):
            return t3[:, k, :]

        block = ctx.enter_context(nc.Block())

        @block.sync
        def _(sp):
            sp.dma_start(C[:, :], const).then_inc(ld_const, 16)
            sp.dma_start(half[:, :], halves).then_inc(ld_const, 16)
            for i in range(2):
                sp.dma_start(X[:, i * 16:(i + 1) * 16, :], x[:, i * 16:(i + 1) * 16, :]).then_inc(ld_x, 16)
            for s in counted:
                sp.sem_inc(s)
            sp.dma_start(W2[0][:, :, :], w2_0).then_inc(ld_w2, 16)
            for e in range(E):
                if e >= 2:
                    sp.wait_ge(w1h, e - 1)
                    sp.wait_ge(w1l, e - 1)
                    sp.wait_ge(bias_ps, e - 1)
                sp.dma_start(raw1[:, e % 2, :], w1gv[e]).then_inc(w1gv_slot[e % 2], 16)
            sp.dma_start(W2[1][:, :, :], w2_1).then_inc(ld_w2, 16)
            with sp.Fori(0, BLOCKS) as i:
                sp.wait_ge(x_moe, ONE + i + BLOCKS + 1)
                sp.dma_start(out[:, bass.ds(i * BT, BT), :], xb(i)).then_inc(stored, 16)
            sp.wait_ge(stored, 16 * BLOCKS)

        def pool_norm(n, s, eps):
            nc.gpsimd.wait_ge(ln[s]["mv"], ONE + n * BT + BT)
            nc.gpsimd.sem_inc(wait_done)
            nc.gpsimd.tensor_scalar(var[s][:, :], mv[s][:, :, 1], eps, None, ALU.add).then_inc(ln[s]["var"], 1)
            nc.gpsimd.wait_ge(ln[s]["var"], ONE + n + 1)
            nc.gpsimd.wait_ge(ln[s]["y"], ONE + n * BT)
            nc.gpsimd.tensor_tensor(rstd[s][:, :], var[s][:, :], con("minus_half"), ALU.pow)\
                .then_inc(ln[s]["rstd"], 1)

        def pool_att(n):
            pool_norm(n, "a", ATT_EPS)
            pool = nc.gpsimd
            pool.wait_ge(q_t, ONE + n + 1)
            pool.wait_ge(att_free, ONE + n * FILLS + FILL["Q"] + 1)
            pool.wait_ge(att_full, ONE + n * FILLS)
            for g in range(4):
                r = slice(32 * g, 32 * g + 32)
                if g:
                    pool.wait_ge(q_m, ONE + n * 4 + g)
                pool.tensor_tensor(Qm[r, g, :], tq[r, 0, :], tq[r, 1, :], ALU.add).then_inc(q_m, 1)
            pool.wait_ge(q_m, ONE + n * 4 + 4)
            pool.wait_ge(k_t, ONE + n + 1)
            pool.wait_ge(att_free, ONE + n * FILLS + FILL["K"] + 1)
            pool.tensor_tensor(kr, tk[:, 0, :], tk[:, 1, :], ALU.add).then_inc(k_r, 1)
            for k in range(BT):
                pool.wait_ge(p_rec, ONE + n * BT + k + 1)
                p = Sx[:, k % 2, :].rearrange("p (h m) -> p h m", h=HEADS)
                pool.tensor_tensor(p, p, srec[:, k, :].unsqueeze(2).to_broadcast([P, HEADS, WIN]), ALU.mult)\
                    .then_inc(p_nrm, 1)

        def pool_prep(n):
            pool_norm(n, "m", TOK_EPS)
            pool = nc.gpsimd
            pool.wait_ge(xh_sb, ONE + n + 1)
            pool.tensor_tensor(xl[:, :], ymT[:, :], xh[:, :].bitcast(F32), ALU.subtract).then_inc(xl_sb, 1)

        def pool_moe(n):
            pool = nc.gpsimd
            for u in range(UNITS):
                pool.wait_ge(h_sb, ONE + n * UNITS + u + 1)
                if u % FT == 0:
                    pool.wait_ge(c_free, ONE + n * E + u // FT + 1)
                if u >= 2:
                    pool.wait_ge(h2_used, ONE + n * UNITS + u - 1)
                else:
                    pool.wait_ge(h2_used, ONE + n * UNITS)
                pool.tensor_tensor(h2[:, u % 2, :], h[:, u % 2, :], csb[:, (u // FT) % 2, :], ALU.mult)\
                    .then_inc(h2_sb, 1)

        @block.gpsimd
        def _(pool):
            for e in range(E):
                if e >= 2:
                    pool.wait_ge(w0l, e - 1)
                    pool.wait_ge(w0h, e - 1)
                pool.dma_start(raw0[:, e % 2, :], w13[:, e, :, :].rearrange("p a f -> p (a f)"))\
                    .then_inc(w13_slot[e % 2], 16)
                if e == 1:
                    pool.memset(region_a[:, :], 0.0).then_inc(setup, 1)
                    pool.wait_ge(ld_const, 32)
            with pool.Fori(0, BLOCKS) as i:
                pool_att(i)
            with pool.Fori(0, BLOCKS) as i:
                pool_prep(i)
                pool_moe(i)
            with pool.Fori(0, BLOCKS) as i:
                pool_norm(i, "c", ATT_EPS)
            pool.wait_ge(newton, 5)
            pool.tensor_tensor(rstrace[:, :], trace[:, :], con("minus_half")[:, 0:1], ALU.pow).then_inc(wh_ready, 1)
            with pool.Fori(0, BLOCKS) as i:
                if True:
                    pool.wait_ge(wh_ps, ONE + i)
                    pool.tensor_copy(fts[:, :], FT_[:, bass.ds(i * BLOCK, BLOCK)]).then_inc(fts_sb, 1)
                pool_prep(i + BLOCKS)
                pool_moe(i + BLOCKS)

        def act_att(n):
            act = nc.scalar
            act.wait_ge(att_full, ONE + n * FILLS + FILL["T"] + 1)
            act.activation(yaT[:, :], bank[:, ATT0, :], ACT.Copy).then_inc(att_free, 1)
            act.wait_ge(k_r, ONE + n + 1)
            for j in range(4):
                act.activation(Kbd[:, :, j, :], kr.rearrange("p (w m) -> p w m", w=BW), ACT.Copy,
                               scale=con("in_quad")[:, j:j + 1]).then_inc(k_bd, 1)
            act.wait_ge(att_full, ONE + n * FILLS + FILL["V"] + 1)
            act.activation(Vp[:, :, :].rearrange("p w c -> p (w c)"), bank[:, ATT0, :], ACT.Copy)\
                .then_inc(att_free, 1)

            def exp(k):
                act.wait_ge(att_free, ONE + n * FILLS + FILL[f"S{k}"] + 1)
                act.activation(Sx[:, k % 2, :], Sx[:, k % 2, :], ACT.Exp).then_inc(p_exp, 1)

            def transposed(k):
                act.wait_ge(att_full, ONE + n * FILLS + FILL[f"T{k}"] + 1)
                act.activation(PT[:, :, :].rearrange("p a n -> p (a n)"),
                               bank[:, ATT0:ATT1 + 1, :].rearrange("p b n -> p (b n)"), ACT.Copy)\
                    .then_inc(att_free, 1)

            def mixed(k):
                act.wait_ge(att_full, ONE + n * FILLS + FILL[f"O{k}"] + 1)
                act.activation(On[:, :, k * P:(k + 1) * P].rearrange("p j (w n) -> p w j n", w=2),
                               bank[:, ATT0, :].rearrange("p (w j n) -> p w j n", w=2, j=4), ACT.Copy)\
                    .then_inc(att_free, 1)

            exp(0)
            exp(1)
            transposed(0)
            mixed(0)
            exp(2)
            transposed(1)
            mixed(1)
            exp(3)
            transposed(2)
            mixed(2)
            transposed(3)
            mixed(3)

        def act_prep(n, layer):
            act = nc.scalar
            act.wait_ge(prep_full, ONE + n * 3 + 1)
            act.activation(ymT[:, :], bank[:, C_BANK, :], ACT.Copy).then_inc(prep_free, 1)
            act.wait_ge(prep_free, ONE + n * 3 + 1)
            act.wait_ge(gu_full, ONE + n * UNITS)
            act.activation(xh[:, :], ymT[:, :], ACT.Copy).then_inc(xh_sb, 1)
            act.wait_ge(l_sub, ONE + n + 1)
            act.activation(lex[:, :, :], lex[:, :, :], ACT.Exp).then_inc(l_exp, 1)
            act.wait_ge(prep_full, ONE + n * 3 + 3)
            gates = bank[0:SPLIT * E, C_BANK, 0:BLOCK // 2].bitcast(BF16)
            act.activation(gT[:, :], gates, ACT.Copy).then_inc(gT_sb, 1)
            act.activation(gTf[:, :], gates, ACT.Copy).then_inc(prep_free, 1)

        def act_moe(n, layer):
            act = nc.scalar
            for u in range(UNITS):
                if u % FT == 0:
                    e = u // FT
                    act.wait_ge(c_full, ONE + n * E + e + 1)
                    if e >= 2:
                        act.wait_ge(h2_sb, ONE + n * UNITS + FT * (e - 1))
                    else:
                        act.wait_ge(h2_sb, ONE + n * UNITS)
                    act.activation(csb[:, e % 2, :], bank[:, C_BANK, :], ACT.Copy).then_inc(c_free, 1)
                act.wait_ge(gu_full, ONE + n * UNITS + u + 1)
                if u >= 2:
                    act.wait_ge(h_sb, ONE + n * UNITS + u - 1)
                else:
                    act.wait_ge(h_sb, ONE + n * UNITS)
                bias = gv_bias[:, u:u + 1] if layer else 0.0
                act.activation(silu[:, u % 2, :], G(u), ACT.Silu, bias=bias).then_inc(g_free, 1)
            act.wait_ge(h2_used, ONE + n * UNITS + UNITS)
            act.activation(ob[:, :], bank[:, ACC_BANK, :], ACT.Copy).then_inc(ob_sb, 1)

        @block.scalar
        def _(act):
            act.dma_start(S[:, :], small).then_inc(ld_small, 16)
            act.dma_start(qkv_w[:, :, :], att_w).then_inc(ld_att, 16)
            act.dma_start(wo[:, :, :], proj_w).then_inc(ld_att, 16)
            for e in range(E):
                act.wait_ge(w13_slot[e % 2], 16 * (e // 2 + 1))
                act.activation(Wh[0][:, e, :], raw0[:, e % 2, :], ACT.Copy).then_inc(w0h, 1)
            for e in range(E):
                act.wait_ge(fold_ps, e + 1)
                act.activation(Wh[1][:, e, :], G(e), ACT.Copy).then_inc(w1h, 1)
            act.wait_ge(ld_const, 32)
            with act.Fori(0, BLOCKS) as i:
                act_att(i)
            with act.Fori(0, BLOCKS) as i:
                act_prep(i, 0)
                act_moe(i, 0)
            with act.Fori(0, BLOCKS) as i:
                act.wait_ge(cov_ps, ONE + i + 1)
                act.activation(FT_[:, bass.ds(i * BLOCK, BLOCK)], bank[:, ATT0, :], ACT.Copy).then_inc(ft_sb, 1)
            with act.Fori(0, BLOCKS) as i:
                act_prep(i + BLOCKS, 1)
                act_moe(i + BLOCKS, 1)

        def dve_norm(n, s, i, y, used, before):
            dve = nc.vector
            before()
            dve.sem_inc(wait_done)
            for k in range(BT):
                nc.vector.bn_stats(stats[s][:, k, :], X[:, bass.ds(i * BT + k, 1), :].rearrange("p a c -> p (a c)"))\
                    .then_inc(ln[s]["stats"], 1)
            dve.wait_ge(ln[s]["var"], ONE + n)
            for k in range(BT):
                dve.wait_ge(ln[s]["stats"], ONE + n * BT + k + 1)
                dve.sem_inc(wait_done)
                nc.vector.bn_aggr(mv[s][:, k, :], stats[s][:, k, :]).then_inc(ln[s]["mv"], 1)
            dve.wait_ge(ln[s]["mv"], ONE + n * BT + BT)
            used()
            dve.wait_ge(ln[s]["rstd"], ONE + n + 1)
            for k in range(BT):
                nc.vector.tensor_scalar(y(k), X[:, bass.ds(i * BT + k, 1), :].rearrange("p a c -> p (a c)"),
                                        mv[s][:, k, 0:1], rstd[s][:, k:k + 1], ALU.subtract, ALU.mult)\
                    .then_inc(ln[s]["y"], 1)

        def dve_att(n):
            dve = nc.vector
            dve_norm(n, "a", n, lambda k: ya[:, k, :],
                     lambda: dve.wait_ge(att_full, ONE + n * FILLS), lambda: None)
            rope = con("rope")

            def rotate(dst, half, col, fill, last, done):
                table = rope[:, col * WIN:(col + 1) * WIN].unsqueeze(1).to_broadcast([P, BW, WIN])
                src = bank[:, ATT0 + half, :].rearrange("p (w m) -> p w m", w=BW)
                ins = nc.vector.scalar_tensor_tensor(
                    out=dst[:, half, :].rearrange("p (w m) -> p w m", w=BW), in0=src,
                    scalar=par("qk_bias")[:, col:col + 1], in1=table, op0=ALU.add, op1=ALU.mult)
                ins.then_inc(att_free if last else done, 1)

            for fill, dst, done, used in (("Q", tq, q_t, (q_m, 4)), ("K", tk, k_t, (k_bd, 4))):
                dve.wait_ge(att_full, ONE + n * FILLS + FILL[fill] + 1)
                dve.wait_ge(used[0], ONE + n * used[1])
                base = 0 if fill == "Q" else 2
                rotate(dst, 0, base, fill, False, done)
                rotate(dst, 1, base + 1, fill, True, done)

            def maximum(k):
                dve.wait_ge(att_full, ONE + n * FILLS + FILL[f"S{k}"] + 1)
                s = bank[:, ATT0:ATT1 + 1, :].rearrange("p b (h m) -> p (b h) m", m=WIN)
                nc.vector.tensor_reduce(smax[:, k, :], s, AXIS_X, ALU.max).then_inc(s_max, 1)
                dve.wait_ge(s_max, ONE + n * BT + k + 1)
                if k >= 2:
                    dve.wait_ge(att_full, ONE + n * FILLS + FILL[f"T{k - 2}"] + 1)
                else:
                    dve.wait_ge(att_full, ONE + n * FILLS)
                ins = nc.vector.tensor_tensor(
                    Sx[:, k % 2, :].rearrange("p (h m) -> p h m", h=HEADS), s,
                    smax[:, k, :].unsqueeze(2).to_broadcast([P, HEADS, WIN]), ALU.subtract)
                ins.then_inc(att_free, 1)

            def sums(k):
                dve.wait_ge(p_exp, ONE + n * BT + k + 1)
                nc.vector.tensor_reduce(ssum[:, k, :], Sx[:, k % 2, :].rearrange("p (h m) -> p h m", h=HEADS),
                                        AXIS_X, ALU.add).then_inc(p_sum, 1)
                dve.wait_ge(p_sum, ONE + n * BT + k + 1)
                nc.vector.reciprocal(srec[:, k, :], ssum[:, k, :]).then_inc(p_rec, 1)

            maximum(0)
            maximum(1)
            sums(0)
            sums(1)
            maximum(2)
            sums(2)
            maximum(3)
            sums(3)
            dve.wait_ge(att_full, ONE + n * FILLS + FILL["J"] + 1)
            nc.vector.tensor_tensor(xb(n), xb(n), att_bias[:, :].unsqueeze(1).to_broadcast([P, BT, P]), ALU.add)\
                .then_inc(x_att, 1)
            dve.wait_ge(x_att, ONE + n + 1)
            nc.vector.tensor_tensor(xb(n), xb(n), bank[:, ATT0, :].rearrange("p (t c) -> p t c", t=BT), ALU.add)\
                .then_inc(att_free, 1)

        def dve_prep(n, i, layer, before):
            dve = nc.vector
            dve_norm(n, "m", i, lambda k: ym[:, k, :],
                     lambda: dve.wait_ge(prep_full, ONE + n * 3), before)
            dve.wait_ge(prep_full, ONE + n * 3 + 2)
            logits = bank[:, C_BANK, 0:BT * E].rearrange("p (t e) -> p t e", t=BT)
            if layer:
                ins = nc.vector.tensor_tensor(lg[:, :, :], logits,
                                              par("router1_bias").unsqueeze(1).to_broadcast([P, BT, E]), ALU.add)
            else:
                ins = nc.vector.tensor_copy(lg[:, :, :], logits)
            ins.then_inc(prep_free, 1)
            dve.wait_ge(prep_free, ONE + n * 3 + 2)
            nc.vector.tensor_reduce(lmax[:, :], lg[:, :, :], AXIS_X, ALU.max).then_inc(l_max, 1)
            other = lg[:, :, :].unsqueeze(2).to_broadcast([P, BT, E, E])
            own = lg[:, :, :].unsqueeze(3).to_broadcast([P, BT, E, E])
            nc.vector.tensor_tensor(cmp1[:, :, :, :], other, own, ALU.is_gt).then_inc(g_one, 1)
            nc.vector.tensor_tensor(cmp2[:, :, :, :], other, own, ALU.is_equal).then_inc(g_one, 1)
            dve.wait_ge(l_max, ONE + n + 1)
            nc.vector.tensor_tensor(lex[:, :, :], lg[:, :, :], lmax[:, :].unsqueeze(2).to_broadcast([P, BT, E]),
                                    ALU.subtract).then_inc(l_sub, 1)
            dve.wait_ge(g_one, ONE + n * 4 + 2)
            flat = cmp2[:, :, :, :].rearrange("p t e f -> p t (e f)")
            nc.vector.tensor_tensor(flat, flat, con("earlier").unsqueeze(1).to_broadcast([P, BT, E * E]), ALU.mult)\
                .then_inc(g_one, 1)
            dve.wait_ge(g_one, ONE + n * 4 + 3)
            nc.vector.tensor_tensor(cmp1[:, :, :, :], cmp1[:, :, :, :], cmp2[:, :, :, :], ALU.add).then_inc(g_one, 1)
            dve.wait_ge(g_one, ONE + n * 4 + 4)
            nc.vector.tensor_reduce(rank[:, :, :], cmp1[:, :, :, :], AXIS_X, ALU.add).then_inc(l_rank, 1)
            dve.wait_ge(l_exp, ONE + n + 1)
            if layer:
                nc.vector.tensor_reduce(gsum[:, :], lex[:, :, :], AXIS_X, ALU.add).then_inc(g_two, 1)
            dve.wait_ge(l_rank, ONE + n + 1)
            nc.vector.scalar_tensor_tensor(out=gate[:, :, :], in0=rank[:, :, :], scalar=1.5, in1=lex[:, :, :],
                                           op0=ALU.is_lt, op1=ALU.mult).then_inc(l_sel, 1)
            dve.wait_ge(l_sel, ONE + n + 1)
            if not layer:
                nc.vector.tensor_reduce(gsum[:, :], gate[:, :, :], AXIS_X, ALU.add).then_inc(g_two, 1)
            dve.wait_ge(g_two, ONE + n + 1)
            nc.vector.reciprocal(lmax[:, :], gsum[:, :]).then_inc(g_rec, 1)
            dve.wait_ge(g_rec, ONE + n + 1)
            nc.vector.tensor_tensor(gate[:, :, :], gate[:, :, :], lmax[:, :].unsqueeze(2).to_broadcast([P, BT, E]),
                                    ALU.mult).then_inc(g_sb, 1)
            dve.wait_ge(g_sb, ONE + n * 6 + 1)
            nc.vector.tensor_copy(g3[:, :, 0, :], gate[:, :, :]).then_inc(g_sb, 1)
            dve.wait_ge(g_sb, ONE + n * 6 + 2)
            nc.vector.tensor_tensor(gres[:, :, :], gate[:, :, :], g3[:, :, 0, :], ALU.subtract).then_inc(g_sb, 1)
            dve.wait_ge(g_sb, ONE + n * 6 + 3)
            nc.vector.tensor_copy(g3[:, :, 1, :], gres[:, :, :]).then_inc(g_sb, 1)
            dve.wait_ge(g_sb, ONE + n * 6 + 4)
            nc.vector.tensor_tensor(gate[:, :, :], gres[:, :, :], g3[:, :, 1, :], ALU.subtract).then_inc(g_sb, 1)
            dve.wait_ge(g_sb, ONE + n * 6 + 5)
            nc.vector.tensor_copy(g3[:, :, 2, :], gate[:, :, :]).then_inc(g_sb, 1)

        def dve_moe(n, i, layer):
            dve = nc.vector
            for u in range(UNITS):
                dve.wait_ge(g_free, ONE + n * UNITS + u + 1)
                if u >= 2:
                    dve.wait_ge(h2_sb, ONE + n * UNITS + u - 1)
                else:
                    dve.wait_ge(h2_sb, ONE + n * UNITS)
                if layer:
                    ins = nc.vector.scalar_tensor_tensor(
                        out=h[:, u % 2, :], in0=U(u), scalar=gv_bias[:, UNITS + u:UNITS + u + 1],
                        in1=silu[:, u % 2, :], op0=ALU.add, op1=ALU.mult)
                else:
                    ins = nc.vector.tensor_tensor(h[:, u % 2, :], silu[:, u % 2, :], U(u), ALU.mult)
                ins.then_inc(h_sb, 1)
            dve.wait_ge(post_full, ONE + n + 1)
            nc.vector.tensor_tensor(xb(i), xb(i), bank[:, ACC_BANK, :].rearrange("p (t c) -> p t c", t=BT), ALU.add)\
                .then_inc(x_moe, 1)

        @block.vector
        def _(dve):
            dve.wait_ge(ld_small, 16)
            dve.wait_ge(ld_const, 32)
            for e in range(E):
                dve.wait_ge(w0h, e + 1)
                nc.vector.tensor_tensor(Wl[0][:, e, :], raw0[:, e % 2, :], Wh[0][:, e, :].bitcast(F32), ALU.subtract)\
                    .then_inc(w0l, 1)
            for e in range(E):
                dve.wait_ge(w1h, e + 1)
                nc.vector.tensor_tensor(Wl[1][:, e, :], G(e), Wh[1][:, e, :].bitcast(F32), ALU.subtract)\
                    .then_inc(w1l, 1)
            dve.wait_ge(bias_ps, E)
            nc.vector.tensor_tensor(gv_bias[:, :], bank[:, ATT0, 0:2 * UNITS], par("gv_bias"), ALU.add)\
                .then_inc(bias_sb, 1)
            dve.wait_ge(abias_ps, 1)
            nc.vector.tensor_tensor(att_bias[:, :], bank[:, ATT1, 0:P], par("proj_bias"), ALU.add).then_inc(abias_sb, 1)
            dve.wait_ge(abias_sb, 1)
            dve.wait_ge(bias_sb, 1)
            dve.wait_ge(ld_x, 32)
            with dve.Fori(0, BLOCKS) as i:
                dve_att(i)
            with dve.Fori(0, BLOCKS) as i:
                dve_prep(i, i, 0, lambda: dve.wait_ge(att_free, ONE + (i + 1) * FILLS))
                dve_moe(i, i, 0)
            with dve.Fori(0, BLOCKS) as i:
                dve_norm(i, "c", i, lambda k: Y2[:, bass.ds(i * BT + k, 1), :].rearrange("p a c -> p (a c)"),
                         lambda: None, lambda: dve.wait_ge(x_moe, ONE + i + 1))
            dve.wait_ge(mean_ps, 1)
            nc.vector.tensor_copy(mean_c[:, :], bank[:, ATT1, 0:P]).then_inc(mean_sb, 1)
            dve.wait_ge(mean_sb, 1)
            with dve.Fori(0, BLOCKS) as i:
                dve.wait_ge(cov_ps, ONE + i)
                nc.vector.tensor_tensor(ya[:, :, :], Y2[:, bass.ds(i * BT, BT), :],
                                        mean_c[:, :].unsqueeze(1).to_broadcast([P, BT, P]), ALU.subtract)\
                    .then_inc(f_sb, 1)
            dve.wait_ge(cov_ps, ONE + BLOCKS)
            step = [0]

            def link(ins):
                ins.then_inc(newton, 1)
                step[0] += 1
                dve.wait_ge(newton, step[0])

            link(nc.vector.scalar_tensor_tensor(out=cov[:, :], in0=bank[:, ATT1, 0:P],
                                                scalar=(1.0 - WHITEN_EPS) / (TOKENS - 1.0), in1=con("same_group"),
                                                op0=ALU.mult, op1=ALU.mult))
            link(nc.vector.scalar_tensor_tensor(out=cov[:, :], in0=ident, scalar=WHITEN_EPS, in1=cov[:, :],
                                                op0=ALU.mult, op1=ALU.add))
            link(nc.vector.tensor_tensor(covd[:, :], cov[:, :], ident, ALU.mult))
            link(nc.vector.tensor_reduce(diag[:, :], covd[:, :], AXIS_X, ALU.add))
            dve.wait_ge(newton_ps, 1)
            link(nc.vector.tensor_copy(trace[:, :], bank[:, ATT0, 0:1]))
            link(nc.vector.reciprocal(rtrace[:, :], trace[:, :]))
            link(nc.vector.tensor_scalar(sig[:, :], cov[:, :], rtrace[:, 0:1], None, ALU.mult))
            link(nc.vector.tensor_scalar(tmpn[:, :], sig[:, :], -0.5, None, ALU.mult))
            link(nc.vector.scalar_tensor_tensor(out=Pm[:, 0, :], in0=ident, scalar=1.5, in1=tmpn[:, :],
                                                op0=ALU.mult, op1=ALU.add))
            for it in range(NEWTON_STEPS - 1):
                old, new = Pm[:, it % 2, :], Pm[:, (it + 1) % 2, :]
                dve.wait_ge(newton_ps, 3 * it + 2)
                link(nc.vector.tensor_copy(N1[:, :], bank[:, ATT0, 0:P]))
                dve.wait_ge(newton_ps, 3 * it + 3)
                link(nc.vector.tensor_copy(N2[:, :], bank[:, ATT1, 0:P]))
                dve.wait_ge(newton_ps, 3 * it + 4)
                link(nc.vector.tensor_scalar(tmpn[:, :], bank[:, ATT0, 0:P], -0.5, None, ALU.mult))
                link(nc.vector.scalar_tensor_tensor(out=new, in0=old, scalar=1.5, in1=tmpn[:, :],
                                                    op0=ALU.mult, op1=ALU.add))
            dve.wait_ge(wh_ready, 1)
            nc.vector.scalar_tensor_tensor(out=whiten[:, :], in0=Pm[:, (NEWTON_STEPS - 1) % 2, :],
                                           scalar=rstrace[:, 0:1], in1=par("gamma"), op0=ALU.mult, op1=ALU.mult)\
                .then_inc(wh_ready, 1)
            with dve.Fori(0, BLOCKS) as i:
                dve.wait_ge(wh_ps, ONE + i + 1)
                nc.vector.tensor_tensor(xb(i), xb(i), bank[:, ATT0, :].rearrange("p (t c) -> p t c", t=BT), ALU.add)\
                    .then_inc(x_wh, 1)
                dve.wait_ge(x_wh, ONE + 2 * i + 1)
                nc.vector.tensor_tensor(xb(i), xb(i), par("beta").unsqueeze(1).to_broadcast([P, BT, P]), ALU.add)\
                    .then_inc(x_wh, 1)
                dve_prep(i + BLOCKS, i, 1, lambda: dve.wait_ge(x_wh, ONE + 2 * i + 2))
                dve_moe(i + BLOCKS, i, 1)

        def fill(n, name):
            nc.tensor.wait_ge(att_free, ONE + n * FILLS + FILL[name])

        def pe_att(n):
            pe, mm = nc.tensor, nc.tensor.matmul
            fill(n, "T")
            pe.wait_ge(ln["a"]["y"], ONE + n * BT + BT)
            for k in range(BT):
                last = nc.tensor.transpose(bank[:, ATT0, k * P:(k + 1) * P], ya[:, k, :], ident)
            last.then_inc(att_full, 1)
            for name, w in (("Q", 0), ("K", 2)):
                fill(n, name)
                mm(bank[:, ATT0, :], qkv_w[:, w, :], yaT[:, :], start=True, stop=True)
                mm(bank[:, ATT1, :], qkv_w[:, w + 1, :], yaT[:, :], start=True, stop=True)\
                    .then_inc(att_full, 1)
            fill(n, "V")
            for w in range(BW):
                for hh in range(2):
                    c = slice(64 * hh, 64 * hh + 64)
                    last = mm(bank[c, ATT0, w * WIN:(w + 1) * WIN], yaT[:, w * WIN:(w + 1) * WIN],
                              qkv_w[:, 4, c], start=True, stop=True)
            last.then_inc(att_full, 1)

            def scores(k):
                fill(n, f"S{k}")
                if k == 0:
                    pe.wait_ge(q_m, ONE + n * 4 + 4)
                    pe.wait_ge(k_bd, ONE + n * 4 + 4)
                for g in range(4):
                    for w in range(2):
                        t = (2 * k + w) * WIN
                        last = mm(bank[w * WIN:(w + 1) * WIN, ATT0 + g // 2, (g % 2) * 256:(g % 2 + 1) * 256],
                                  Qm[:, g, t:t + WIN], Kbd[:, 2 * k + w, :, :].rearrange("p j m -> p (j m)"),
                                  start=True, stop=True)
                last.then_inc(att_full, 1)

            def turned(k):
                fill(n, f"T{k}")
                pe.wait_ge(p_nrm, ONE + n * BT + k + 1)
                for a in range(HP):
                    last = nc.tensor.transpose(bank[:, ATT0 + a // 4, (a % 4) * P:(a % 4 + 1) * P],
                                               Sx[:, k % 2, a * P:(a + 1) * P], ident)
                last.then_inc(att_full, 1)

            def values(k):
                fill(n, f"O{k}")
                pe.sem_inc(wait_done)
                for w in range(2):
                    for q in range(2):
                        for hh in range(2):
                            r, o = slice(64 * hh, 64 * hh + 64), 32 * (2 * hh + q)
                            last = mm(bank[o:o + 32, ATT0, w * 256:(w + 1) * 256],
                                      Vp[r, 2 * k + w, q * 32:(q + 1) * 32],
                                      PT[r, 4 * q:4 * q + 4, w * WIN:(w + 1) * WIN], start=True, stop=True)
                last.then_inc(att_full, 1)

            scores(0)
            scores(1)
            turned(0)
            values(0)
            scores(2)
            turned(1)
            values(1)
            scores(3)
            turned(2)
            values(2)
            turned(3)
            values(3)
            fill(n, "J")
            for k in range(BT):
                for j in range(4):
                    last = mm(bank[:, ATT0, k * P:(k + 1) * P], On[:, j, k * P:(k + 1) * P], wo[:, j, :],
                              start=(j == 0), stop=(j == 3))
            last.then_inc(att_full, 1)

        def pe_prep(n, layer):
            pe, mm = nc.tensor, nc.tensor.matmul
            pe.wait_ge(prep_free, ONE + n * 3)
            pe.wait_ge(c_free, ONE + n * E)
            pe.wait_ge(ln["m"]["y"], ONE + n * BT + BT)
            for k in range(BT):
                last = nc.tensor.transpose(bank[:, C_BANK, k * P:(k + 1) * P], ym[:, k, :], ident)
            last.then_inc(prep_full, 1)
            pe.wait_ge(prep_free, ONE + n * 3 + 1)
            for k in range(BT):
                last = mm(bank[:, C_BANK, k * E:(k + 1) * E], ymT[:, k * P:(k + 1) * P],
                          par(f"router{layer}"), start=True, stop=True)
            last.then_inc(prep_full, 1)
            pe.wait_ge(prep_free, ONE + n * 3 + 2)
            pe.wait_ge(g_sb, ONE + n * 6 + 6)
            gates = bank[0:SPLIT * E, C_BANK, 0:BLOCK // 2].bitcast(BF16)
            for k in range(BT):
                last = nc.tensor.transpose(gates[:, k * P:(k + 1) * P],
                                           g3[:, k, :, :].rearrange("p s e -> p (s e)"), ident_b)
            last.then_inc(prep_full, 1)

        def pe_moe(n, layer):
            pe, mm = nc.tensor, nc.tensor.matmul

            def down(u):
                pe.wait_ge(h2_sb, ONE + n * UNITS + u + 1)
                if u == 0:
                    pe.wait_ge(x_moe, ONE + n)
                    if layer:
                        pe.wait_ge(prep_free, ONE + n * 3 + 3)
                        mm(bank[:, ACC_BANK, :], par("b2")[0:SPLIT * E, :], gTf[:, :], start=True, stop=False)
                mm(bank[:, ACC_BANK, :], W2[layer][:, u, :], h2[:, u % 2, :],
                   start=(u == 0 and not layer), stop=(u == UNITS - 1)).then_inc(h2_used, 1)

            for u in range(UNITS):
                e, ft = u // FT, u % FT
                if ft == 0:
                    pe.wait_ge(c_free, ONE + n * E + e)
                    if e == 0:
                        pe.wait_ge(prep_free, ONE + n * 3 + 3)
                        pe.wait_ge(xl_sb, ONE + n + 1)
                    mm(bank[:, C_BANK, :], select[:, e, :], gT[:, :], start=True, stop=True).then_inc(c_full, 1)
                if u >= 2:
                    pe.wait_ge(h_sb, ONE + n * UNITS + u - 1)
                else:
                    pe.wait_ge(h_sb, ONE + n * UNITS)
                for part, dst in ((0, G(u)), (1, U(u))):
                    c = part * FF + ft * P
                    wh, wl = Wh[layer][:, e, c:c + P], Wl[layer][:, e, c:c + P]
                    mm(dst, wh, xh[:, :], start=True, stop=False)
                    mm(dst, wh, xl[:, :], start=False, stop=False)
                    last = mm(dst, wl, xh[:, :], start=False, stop=True)
                last.then_inc(gu_full, 1)
                if u >= 1:
                    down(u - 1)
            down(UNITS - 1)

        def pe_post(n):
            pe = nc.tensor
            pe.wait_ge(ob_sb, ONE + n + 1)
            for k in range(BT):
                last = nc.tensor.transpose(bank[:, ACC_BANK, k * P:(k + 1) * P], ob[:, k * P:(k + 1) * P], ident)
            last.then_inc(post_full, 1)

        @block.tensor
        def _(pe):
            mm = nc.tensor.matmul
            pe.wait_ge(ld_small, 16)
            for e in range(E):
                pe.wait_ge(w1gv_slot[e % 2], 16 * (e // 2 + 1))
                if e >= 2:
                    pe.wait_ge(w1l, e - 1)
                raw = raw1[:, e % 2, :]
                for ht in range(FT):
                    last = mm(G(e), raw[:, ht * P:(ht + 1) * P], raw[:, FF + ht * 2 * FF:FF + (ht + 1) * 2 * FF],
                              start=(ht == 0), stop=(ht == FT - 1))
                last.then_inc(fold_ps, 1)
                for part in range(2):
                    for ft in range(FT):
                        col = part * UNITS + e * FT + ft
                        for ht in range(FT):
                            c = FF + ht * 2 * FF + part * FF + ft * P
                            last = mm(bank[:, ATT0, col:col + 1], raw[:, c:c + P],
                                      par("b1")[:, e * FT + ht:e * FT + ht + 1], start=(ht == 0), stop=(ht == FT - 1))
                last.then_inc(bias_ps, 1)
            pe.wait_ge(ld_att, 32)
            mm(bank[:, ATT1, 0:P], par("v_bias"), wo[:, 4, :], start=True, stop=True).then_inc(abias_ps, 1)
            pe.wait_ge(abias_sb, 1)
            pe.wait_ge(bias_sb, 1)
            pe.wait_ge(setup, 1)
            pe.wait_ge(ld_const, 32)
            with pe.Fori(0, BLOCKS) as i:
                pe_att(i)
            pe.wait_ge(w0l, E)
            pe.wait_ge(w0h, E)
            pe.wait_ge(ld_w2, 32)
            with pe.Fori(0, BLOCKS) as i:
                pe_prep(i, 0)
                pe_moe(i, 0)
                pe_post(i)
            pe.wait_ge(att_free, ONE + BLOCKS * FILLS)
            for t in range(TILES):
                if t % BT == 0:
                    pe.wait_ge(ln["c"]["y"], ONE + t + BT)
                last = mm(bank[:, ATT1, 0:P], con("mean"), Y2[:, t, :], start=(t == 0), stop=(t == TILES - 1))
            last.then_inc(mean_ps, 1)

            def covariance(i, first, final):
                pe.wait_ge(ft_sb, ONE + i)
                pe.wait_ge(f_sb, ONE + i + 1)
                for k in range(BT):
                    mm(bank[:, ATT1, 0:P], ya[:, k, :], ya[:, k, :], start=(first and k == 0),
                       stop=(final and k == BT - 1))
                for k in range(BT):
                    last = nc.tensor.transpose(bank[:, ATT0, k * P:(k + 1) * P], ya[:, k, :], ident)
                last.then_inc(cov_ps, 1)

            pe.wait_ge(mean_sb, 1)
            covariance(0, True, False)
            with pe.Fori(1, BLOCKS - 1) as i:
                covariance(i, False, False)
            covariance(BLOCKS - 1, False, True)
            pe.wait_ge(ft_sb, ONE + BLOCKS)
            pe.wait_ge(newton, 4)
            mm(bank[:, ATT0, 0:1], con("same_group"), diag[:, :], start=True, stop=True).then_inc(newton_ps, 1)
            for it in range(NEWTON_STEPS - 1):
                old = Pm[:, it % 2, :]
                pe.wait_ge(newton, 9 + 4 * it)
                mm(bank[:, ATT0, 0:P], old, old, start=True, stop=True).then_inc(newton_ps, 1)
                pe.wait_ge(newton, 10 + 4 * it)
                mm(bank[:, ATT1, 0:P], N1[:, :], old, start=True, stop=True).then_inc(newton_ps, 1)
                pe.wait_ge(newton, 11 + 4 * it)
                mm(bank[:, ATT0, 0:P], N2[:, :], sig[:, :], start=True, stop=True).then_inc(newton_ps, 1)
            pe.wait_ge(wh_ready, 2)
            with pe.Fori(0, BLOCKS) as i:
                pe.wait_ge(fts_sb, ONE + i + 1)
                pe.wait_ge(x_wh, ONE + 2 * i)
                for k in range(BT):
                    last = mm(bank[:, ATT0, k * P:(k + 1) * P], fts[:, k * P:(k + 1) * P], whiten[:, :],
                              start=True, stop=True)
                last.then_inc(wh_ps, 1)
                pe_prep(i + BLOCKS, 1)
                pe_moe(i + BLOCKS, 1)
                pe_post(i + BLOCKS)


def _tokens(x):
    return x.reshape(8, 8, 2, 2, 8, 2, P).transpose(5, 1, 4, 0, 3, 2, 6).reshape(P, TILES, P)


def _image(y):
    return y.reshape(2, 8, 8, 8, 2, 2, P).transpose(3, 1, 5, 4, 2, 0, 6).reshape(4, 32, 32, P)


def _columns(width, at, **arrays):
    table = np.zeros((P, width), np.float32)
    for name, a in arrays.items():
        col, w = at[name]
        table[:a.shape[0], col:col + w] = a
    return table


def _layout(i):
    ch = np.arange(P)
    swapped = ch ^ 1
    by_parity = np.array([(2 * hp + hh) * HD + d for hh in range(2) for hp in range(HP) for d in range(HD)])
    qw, kw, vw = i["L0_conv_qkv_w"].reshape(3, P, P)
    qb, kb, vb = i["L0_conv_qkv_b"].reshape(3, P)
    att_w = np.stack([qw.T, qw[swapped].T, kw.T, kw[swapped].T, vw[by_parity].T], 1)
    pw = i["L0_conv_proj_w"][:, by_parity].T
    place = (ch // HD) % 4
    masked = [np.where((place == j)[:, None], pw, np.float32(0)) for j in range(4)]
    proj_w = np.stack(masked + [pw], 1)
    row = lambda a: np.broadcast_to(a.reshape(1, -1), (P, a.size))
    cols = lambda a: a.reshape(E * FT, P).T
    small = _columns(
        SMALL_WIDTH, SMALL_AT,
        qk_bias=np.stack([qb, qb[swapped], kb, kb[swapped]], 1),
        v_bias=np.broadcast_to(vb[by_parity][:, None], (P, P)),
        proj_bias=row(i["L0_conv_proj_b"]),
        router0=i["L0_ffn_router_w"], router1=i["L1_ffn_router_w"], router1_bias=row(i["L1_ffn_router_b"]),
        gamma=row(i["L1_conv_gamma"]), beta=row(i["L1_conv_beta"]),
        b1=cols(i["L1_ffn_b1"]), gv_bias=np.concatenate([cols(i["L1_ffn_bg"]), cols(i["L1_ffn_bv"])], 1),
        b2=np.concatenate([i["L1_ffn_b2"]] * SPLIT, 0))
    w13 = np.stack([i["L0_ffn_w1"], i["L0_ffn_w3"]], 1).transpose(2, 0, 1, 3)
    down = lambda w: w.reshape(E * FT, P, P).transpose(1, 0, 2)
    w1T = i["L1_ffn_w1"].reshape(E, P, FT, P).transpose(0, 3, 2, 1).reshape(E, P, FT * P)
    gv = np.concatenate([i["L1_ffn_wg"], i["L1_ffn_wv"]], 2).reshape(E, FT, P, 2 * FF).transpose(0, 2, 1, 3)
    return {
        "x": _tokens(i["x"]),
        "const": _columns(CONST_WIDTH, CONST_AT, **constants()),
        "halves": half_constants(),
        "small": small, "att_w": att_w, "proj_w": proj_w, "w13": w13, "w2_0": down(i["L0_ffn_w2"]),
        "w1gv": np.concatenate([w1T, gv.reshape(E, P, FT * 2 * FF)], 2), "w2_1": down(i["L1_ffn_w2"]),
    }


def kernel(**inputs):
    import concourse.bacc as bacc
    from concourse.bass_utils import run_bass_kernel_spmd

    arrays = {k: np.ascontiguousarray(v) for k, v in _layout({k: np.asarray(v) for k, v in inputs.items()}).items()}
    nc = bacc.Bacc("TRN2", target_bir_lowering=False, num_devices=1)
    aps = {k: nc.dram_tensor(f"{k}_dram", v.shape, mybir.dt.from_np(v.dtype), kind="ExternalInput").ap() for k, v in arrays.items()}
    out = nc.dram_tensor("out_dram", (P, TILES, P), F32, kind="ExternalOutput").ap()
    build(nc, out=out, **aps)
    r = run_bass_kernel_spmd(nc, [{f"{k}_dram": v for k, v in arrays.items()}], core_ids=[0])
    return _image(r.results[0]["out_dram"])
```

```python
import numpy as np
import concourse.bass as bass
from concourse import mybir
from contextlib import ExitStack

F32 = mybir.dt.float32
F32R = mybir.dt.float32r
BF16 = mybir.dt.bfloat16
ALU = mybir.AluOpType
ACT = mybir.ActivationFunctionType
AXIS_X = mybir.AxisListType.X

START = 4
P = 128
TOKENS = 4 * 32 * 32
TILES = TOKENS // P
BLOCK = 512
BLOCKS = TOKENS // BLOCK
BT = BLOCK // P
WIN = 64
BW = BLOCK // WIN
HEADS, HD = 16, 8
HP = HEADS // 2
E, FF = 8, 256
FT = FF // P
UNITS = E * FT
GROUPS, MEMBERS = 4, 32
SPLIT = 3
ATT_EPS, TOK_EPS, WHITEN_EPS = 1e-6, 1e-5, 1e-7
NEWTON_STEPS = 3


def constants():
    ch = np.arange(P)
    d = ch % HD
    head = ch // HD
    half = HD // 2
    inv = 1.0 / 10000.0 ** (2 * ((d % half) // 2) / half)
    n = np.arange(WIN)
    place = np.where(d[:, None] < half, n[None, :] // 8, n[None, :] % 8)
    ang = place * inv[:, None]
    cos, sin = np.cos(ang), np.sin(ang) * np.where(d % 2, 1.0, -1.0)[:, None]
    scale = HD ** -0.5
    e = np.arange(E)
    return {
        "ident": np.eye(P),
        "rope": np.concatenate([cos * scale, sin * scale, cos, sin], 1),
        "in_quad": (head[:, None] % 4 == np.arange(4)[None, :]),
        "earlier": np.broadcast_to((e[None, :] < e[:, None]).reshape(1, E * E), (P, E * E)),
        "block_mean": np.full((P, P), 1.0 / BLOCK),
        "same_group": (ch[:, None] // MEMBERS == ch[None, :] // MEMBERS),
        "minus_half": np.full((P, BT), -0.5),
    }


def half_constants():
    sel = np.zeros((P, E, P))
    for r in range(SPLIT * E):
        sel[r, r % E] = 1.0
    one = np.uint16(0x3F80)
    return np.concatenate([np.eye(P), sel.reshape(P, E * P)], 1).astype(np.uint16) * one


CONST_AT, CONST_WIDTH = {}, 0
for _name, _table in constants().items():
    CONST_AT[_name] = (CONST_WIDTH, _table.shape[1])
    CONST_WIDTH += _table.shape[1]

SMALL_AT, SMALL_WIDTH = {}, 0
for _name, _width in (("qk_bias", 4), ("v_bias", P), ("proj_bias", P), ("router0", E), ("router1", E),
                      ("router1_bias", E), ("gamma", P), ("beta", P), ("b1", UNITS), ("gv_bias", 2 * UNITS),
                      ("b2", P)):
    SMALL_AT[_name] = (SMALL_WIDTH, _width)
    SMALL_WIDTH += _width


RAW_SLOTS = 3
DOWN_LAG = 2
ATT_AT = 5
ATT_STEP = {"T": 2, "Q": 3, "K": 4, "V": 5, "S0": 6, "S1": 7, "S2": 8, "T0": 9, "O0": 10, "S3": 10, "T1": 11,
            "O1": 12, "T2": 13, "O2": 14, "T3": 15, "O3": 16, "J": 17}
ATT_LATE = ("S2", "S3", "T1")
ATT_FILL = {name: k for k, name in enumerate(ATT_STEP)}
ATT_FILLS = len(ATT_FILL)
EXP_STEP = (7, 8, 10, 11)
PREP_SLOT = [{"ln": 7, "y": 8, "turn": 9, "route": 10, "rank": 10, "exp": 12, "gates": 13, "gate_rows": 15},
             {"centre": 0, "wturn": 1, "whiten": 3, "ln": 4, "y": 5, "turn": 7, "route": 9, "rank": 9, "exp": 10,
              "gates": 11, "gate_rows": 13}]
POST_SLOT = 2
COV_SLOT = {"ln": 3, "y": 4, "mean": 5, "cov": 7}


def side_fills(layer, experts=True, post=False, cov=False, prep=False):
    order = []
    for s in range(UNITS):
        if experts and s % FT == 0:
            order.append(f"C{s // FT}")
        if post and s == POST_SLOT:
            order.append("post")
        if cov:
            order += [k for k in ("mean", "cov") if COV_SLOT[k] == s]
        if prep:
            order += [k for k in ("turn", "route", "gate_rows") if PREP_SLOT[layer][k] == s]
    return order


class Span:

    def __init__(self, n, p, layer, base, experts=True, post=False, cov=False, prep=None, att=None, att_tail=None,
                 setup=None, folds=None):
        self.n, self.p, self.layer, self.base, self.experts = n, p, layer, base, experts
        self.post, self.cov, self.prep, self.att, self.att_tail = post, cov, prep, att, att_tail
        self.setup = setup
        self.folds = folds or {}
        self.fills = side_fills(layer, experts, post, cov, prep is not None)

    def before(self, name):
        return self.base + self.fills.index(name)

    def attention(self, s):
        steps = []
        if self.att_tail is not None:
            steps.append((self.att_tail, s + UNITS - ATT_AT))
        if self.att is not None and s >= ATT_AT:
            steps.append((self.att, s - ATT_AT))
        return steps

    def first(self, n):
        return isinstance(self.n, int) and self.n == n


def schedule(engine_loop, emit):
    emit(Span(0, 0, 0, 0, experts=False, att=0, setup=-ATT_AT))
    emit(Span(0, 0, 0, 0, experts=False, prep=0, att=1, att_tail=0, setup=UNITS - ATT_AT))
    emit(Span(0, 0, 0, 3, prep=1, att=2, att_tail=1))
    per = len(side_fills(0, True, True, True, True))
    with engine_loop(1, 4, 2) as i:
        for k in range(2):
            n = i + k
            emit(Span(n, (1 + k) % 2, 0, n * per, post=True, cov=True, prep=n + 1, att=n + 2, att_tail=n + 1))
    emit(Span(5, 1, 0, 5 * per, post=True, cov=True, prep=6, att=7, att_tail=6))
    emit(Span(6, 0, 0, 6 * per, post=True, cov=True, prep=7, att_tail=7))
    emit(Span(7, 1, 0, 7 * per, post=True, cov=True))
    emit(Span(8, 0, 0, 7 * per + 11, experts=False, post=True, cov=True, folds={3: 0}))


def schedule_1(engine_loop, emit):
    base = 8 * len(side_fills(0, True, True, True, True))
    emit(Span(8, 0, 1, base, experts=False, prep=8, folds={0: 6, 4: 7}))
    emit(Span(8, 0, 1, base + 3, prep=9))
    base += 3 + len(side_fills(1, prep=True))
    per = len(side_fills(1, post=True, prep=True))
    with engine_loop(9, 14, 2) as i:
        for k in range(2):
            n = i + k
            emit(Span(n, (1 + k) % 2, 1, n * per + (base - 9 * per), post=True, prep=n + 1))
    emit(Span(15, 1, 1, 15 * per + (base - 9 * per), post=True))
    emit(Span(16, 0, 1, 15 * per + (base - 9 * per) + len(side_fills(1, post=True)), experts=False, post=True))


def build(nc, x, const, halves, small, att_w, proj_w, w13, w2_0, w1gv, w2_1, out):
    ctx = ExitStack()
    with ctx:
        def sb(name, shape, dt=F32):
            return ctx.enter_context(nc.sbuf_tensor(name, shape, dt))

        def sem(name):
            return ctx.enter_context(nc.semaphore(name))

        counted = []

        def csem(name):
            counted.append(sem(name))
            return counted[-1]

        def after(engine, semaphore, count):
            if not isinstance(count, int) or count > 0:
                engine.wait_ge(semaphore, START + count)

        X = sb("X", [P, TILES, P])
        C = sb("C", [P, CONST_WIDTH])
        S = sb("S", [P, SMALL_WIDTH])
        qkv_w = sb("qkv_w", [P, 5, P])
        wo = sb("wo", [P, 5, P])
        half = sb("half", [P, P + E * P], mybir.dt.uint16)
        ident_b = half[:, 0:P].bitcast(BF16)
        select = half[0:SPLIT * E, P:P + E * P].bitcast(BF16).rearrange("r (e c) -> r e c", e=E)
        att_bias = sb("att_bias", [P, P])
        Wh = [sb(f"Wh{l}", [P, E, 2 * FF], F32R) for l in range(2)]
        Wl = [sb(f"Wl{l}", [P, E, 2 * FF], F32R) for l in range(2)]
        W2 = [sb(f"W2_{l}", [P, UNITS, P]) for l in range(2)]
        gv_bias = sb("gv_bias", [P, 2 * UNITS])
        Qm = sb("Qm", [P, 4, BLOCK])
        region = sb("region", [P, 8 * BLOCK])
        Kbd = region[:, 0:4 * BLOCK].rearrange("p (w j m) -> p w j m", w=BW, j=4)
        On = region[:, 4 * BLOCK:].rearrange("p (j t) -> p j t", j=4)
        RAW = FT * (P + 2 * FF)
        raw1 = region[:, 0:RAW_SLOTS * RAW].rearrange("p (s n) -> p s n", s=RAW_SLOTS)
        Sx = sb("Sx", [P, 3, HEADS * WIN])
        tq = sb("tq", [P, 2, BLOCK])
        tk = sb("tk", [P, 2, BLOCK])
        kr = tk[:, 0, :]
        PT = sb("PT", [P, HP, P])
        Vp = sb("Vp", [P, BW, HP * HD])
        ya = sb("ya", [P, BT, P])
        yaT = sb("yaT", [P, BLOCK])
        smax = sb("smax", [P, BT, HEADS])
        ssum = sb("ssum", [P, BT, HEADS])
        srec = sb("srec", [P, BT, HEADS])
        stats = {n: sb(f"stats_{n}", [P, BT, 6]) for n in "amc"}
        mv = {n: sb(f"mv_{n}", [P, BT, 2]) for n in "amc"}
        var = {n: sb(f"var_{n}", [P, BT]) for n in "amc"}
        rstd = {n: sb(f"rstd_{n}", [P, BT]) for n in "amc"}
        eps = sb("eps", [P, 3, BT])
        ym = sb("ym", [P, BT, P])
        ymT = sb("ymT", [P, BLOCK])
        xh = sb("xh", [P, 2, BLOCK], F32R)
        xl = sb("xl", [P, 2, BLOCK], F32R)
        lg = sb("lg", [P, BT, E])
        lmax = sb("lmax", [P, BT])
        lex = sb("lex", [P, BT, E])
        cmp1 = sb("cmp1", [P, BT, E, E])
        cmp2 = sb("cmp2", [P, BT, E, E])
        rank = sb("rank", [P, BT, E])
        gsum = sb("gsum", [P, BT])
        gate = sb("gate", [P, BT, E])
        gres = sb("gres", [P, BT, E])
        g3 = sb("g3", [P, BT, SPLIT, E], BF16)
        gT = sb("gT", [SPLIT * E, 2, BLOCK], BF16)
        gTf = Sx[0:SPLIT * E, 0:2, 0:BLOCK]
        work = sb("work", [P, 10, BLOCK])
        csb, silu, h = (work[:, 2 * k:2 * k + 2, :] for k in range(3))
        h2 = work[:, 6:10, :]
        raw0 = work[:, 6:8, :]
        ob = sb("ob", [P, BLOCK])
        yc = sb("yc", [P, BT, P])
        keep = sb("keep", [P, TILES, 2])
        means = sb("means", [P, P])
        cov_acc = sb("cov_acc", [P, P])
        diag, trace, rtrace, rstrace = (sb(n, [P, 1]) for n in ("diag", "trace", "rtrace", "rstrace"))
        matrices = Qm[:, 0:2, :].rearrange("p g (a c) -> p (g a) c", c=P)
        mean_c, cov, covd, sig, N1, tmpn = (matrices[:, k, :] for k in range(6))
        Pm = matrices[:, 6:8, :]
        N2, whiten = covd, cov
        fts = yaT

        def con(name):
            a, w = CONST_AT[name]
            return C[:, a:a + w]

        def par(name):
            a, w = SMALL_AT[name]
            return S[:, a:a + w]

        ident = con("ident")
        bank = ctx.enter_context(nc.psum_tensor("bank", [P, 8, 512], F32))
        SIDE, ACC, ATT0, ATT1 = 4, 5, 6, 7

        def G(u):
            return bank[:, 2 * (u % 2), :]

        def U(u):
            return bank[:, 2 * (u % 2) + 1, :]

        ld_const, ld_small, ld_att, ld_x0, ld_x1, ld_w2 = (sem(f"ld_{n}") for n in (
            "const", "small", "att", "x0", "x1", "w2"))
        w13_slot = [sem(f"w13_slot{k}") for k in range(2)]
        w1gv_slot = [sem(f"w1gv_slot{k}") for k in range(RAW_SLOTS)]
        setup = sem("setup")
        w0h, w0l = sem("w0h"), sem("w0l")
        fold_ps, w1h, w1l = sem("fold_ps"), sem("w1h"), sem("w1l")
        bias_ps, bias_sb = sem("bias_ps"), sem("bias_sb")
        abias_ps, abias_sb = sem("abias_ps"), sem("abias_sb")
        ln = {n: {k: csem(f"{k}_{n}") for k in ("stats", "mv", "var", "rstd", "y")} for n in "amc"}
        att_full, att_free = csem("att_full"), csem("att_free")
        side_full, side_free = csem("side_full"), csem("side_free")
        q_t, q_m, k_t, k_r, k_bd = (csem(n) for n in ("q_t", "q_m", "k_t", "k_r", "k_bd"))
        s_max, p_exp, p_sum, p_rec, p_nrm, x_bias = (csem(n) for n in (
            "s_max", "p_exp", "p_sum", "p_rec", "p_nrm", "x_bias"))
        xh_sb, xl_sb, l_max, l_sub, l_exp, l_cmp, l_rank, l_sel, g_sum, g_rec, g_sb, gTf_sb = (
            csem(n) for n in ("xh_sb", "xl_sb", "l_max", "l_sub", "l_exp", "l_cmp", "l_rank",
                              "l_sel", "g_sum", "g_rec", "g_sb", "gTf_sb"))
        gu_full, g_read, h_sb, h2_sb, h2_used = (csem(n) for n in (
            "gu_full", "g_read", "h_sb", "h2_sb", "h2_used"))
        ob_sb, x_moe = csem("ob_sb"), csem("x_moe")
        f_sb, mean_row, cov_sum, kept = csem("f_sb"), csem("mean_row"), csem("cov_sum"), csem("kept")
        newton, newton_ps, centre_d, wh_ready = sem("newton"), sem("newton_ps"), sem("centre_d"), sem("wh_ready")
        wy_sb, wf_sb, wt_ps, fts_sb, wh_ps, x_beta, x_wh = (csem(n) for n in (
            "wy_sb", "wf_sb", "wt_ps", "fts_sb", "wh_ps", "x_beta", "x_wh"))
        stored = sem("stored")
        wait_done = sem("wait_done")

        TRACE_STEP, FIRST_STEP = 7, 11

        def xb(i):
            return X[:, bass.ds(i * BT, BT), :]

        def xt(i, k):
            return X[:, bass.ds(i * BT + k, 1), :].rearrange("p a c -> p (a c)")

        def over_tiles(row):
            return row.unsqueeze(1).to_broadcast([P, BT, P])

        def stream_block(n, layer):
            return n - BLOCKS if layer else n

        block = ctx.enter_context(nc.Block())

        @block.sync
        def _(sp):
            sp.dma_start(X[:, 0:BT, :], x[:, 0:BT, :]).then_inc(ld_x0, 16)
            sp.dma_start(C[:, :], const).then_inc(ld_const, 16)
            sp.dma_start(half[:, :], halves).then_inc(ld_const, 16)
            for s in counted:
                sp.sem_inc(s, START)
            sp.dma_start(X[:, BT:, :], x[:, BT:, :]).then_inc(ld_x1, 16)
            sp.dma_start(W2[0][:, :, :], w2_0).then_inc(ld_w2, 16)
            sp.dma_start(W2[1][:, :, :], w2_1).then_inc(ld_w2, 16)
            after(sp, att_free, BLOCKS * ATT_FILLS)
            for e in range(E):
                if e >= RAW_SLOTS:
                    sp.wait_ge(bias_ps, e - RAW_SLOTS + 1)
                sp.dma_start(raw1[:, e % RAW_SLOTS, :], w1gv[e]).then_inc(w1gv_slot[e % RAW_SLOTS], 16)
            with sp.Fori(0, BLOCKS) as i:
                after(sp, x_moe, i + (BLOCKS + 1))
                sp.dma_start(out[:, bass.ds(i * BT, BT), :], xb(i)).then_inc(stored, 16)
            sp.wait_ge(stored, 16 * BLOCKS)

        def pool_norm(n, s):
            pool = nc.gpsimd
            after(pool, ln[s]["mv"], n * BT + BT)
            pool.tensor_tensor(var[s][:, :], mv[s][:, :, 1], eps[:, "amc".index(s), :], ALU.add)\
                .then_inc(ln[s]["var"], 1)
            after(pool, ln[s]["var"], n + 1)
            after(pool, ln[s]["y"], n * BT)
            if s == "c":
                after(pool, kept, 2 * n)
            pool.tensor_tensor(rstd[s][:, :], var[s][:, :], con("minus_half"), ALU.pow)\
                .then_inc(ln[s]["rstd"], 1)

        def pool_att(n, s):
            pool = nc.gpsimd
            if s == 0:
                pool_norm(n, "a")
            if s == 2:
                if isinstance(n, int) and n == 0:
                    pool.wait_ge(abias_sb, 1)
                after(pool, ln["a"]["y"], n * BT + BT)
                pool.tensor_tensor(xb(n), xb(n), over_tiles(att_bias[:, :]), ALU.add).then_inc(x_bias, 1)
            if s == ATT_STEP["Q"]:
                after(pool, q_t, n + 1)
                after(pool, att_free, n * ATT_FILLS + ATT_FILL["Q"] + 1)
                for g in range(4):
                    r = slice(32 * g, 32 * g + 32)
                    after(pool, q_m, n * 4 + g)
                    pool.tensor_tensor(Qm[r, g, :], tq[r, 0, :], tq[r, 1, :], ALU.add).then_inc(q_m, 1)
                after(pool, q_m, n * 4 + 4)
            if s == ATT_STEP["K"]:
                after(pool, k_t, n + 1)
                after(pool, att_free, n * ATT_FILLS + ATT_FILL["K"] + 1)
                pool.tensor_tensor(kr, tk[:, 0, :], tk[:, 1, :], ALU.add).then_inc(k_r, 1)
            for k, at in enumerate(EXP_STEP):
                if s == at:
                    after(pool, p_rec, n * BT + k + 1)
                    p = Sx[:, k % 3, :].rearrange("p (h m) -> p h m", h=HEADS)
                    pool.tensor_tensor(p, p, srec[:, k, :].unsqueeze(2).to_broadcast([P, HEADS, WIN]), ALU.mult)\
                        .then_inc(p_nrm, 1)

        def pool_prep(n, s, layer, p):
            pool, at = nc.gpsimd, PREP_SLOT[layer]
            if layer and s == at["wturn"]:
                i = n - BLOCKS
                after(pool, wy_sb, i * BT + BT)
                pool.tensor_tensor(xb(i), xb(i), over_tiles(par("beta")), ALU.add).then_inc(x_beta, 1)
            if s == at["ln"]:
                pool_norm(n, "m")
            if s == at["turn"]:
                after(pool, xh_sb, n + 1)
                pool.tensor_tensor(xl[:, p, :], ymT[:, :], xh[:, p, :].bitcast(F32), ALU.subtract)\
                    .then_inc(xl_sb, 1)

        def pool_unit(sp, n, u):
            pool = nc.gpsimd
            after(pool, h_sb, n * UNITS + (u + 1))
            if u % FT == 0:
                after(pool, side_free, sp.before(f"C{u // FT}") + 1)
            after(pool, h2_used, n * UNITS + (u - 3))
            pool.tensor_tensor(h2[:, u % 4, :], h[:, u % 2, :], csb[:, (u // FT) % 2, :], ALU.mult)\
                .then_inc(h2_sb, 1)

        def pool_span(sp):
            for s in range(UNITS):
                if sp.experts:
                    pool_unit(sp, sp.n, s)
                for n, a in sp.attention(s):
                    pool_att(n, a)
                if sp.cov and s == COV_SLOT["ln"]:
                    pool_norm(sp.n - 1, "c")
                if sp.prep is not None:
                    pool_prep(sp.prep, s, sp.layer, sp.p if not sp.experts else 1 - sp.p)
                if sp.setup is not None and 0 <= sp.setup + s < UNITS:
                    pool_setup(sp.setup + s)

        def pool_setup(s):
            pool, e = nc.gpsimd, s // 2 + 2
            if s % 2 and e < E:
                pool.wait_ge(w0l, e - 1)
                pool.dma_start(raw0[:, e % 2, :], w13[:, e, :, :].rearrange("p a f -> p (a f)"))\
                    .then_inc(w13_slot[e % 2], 16)

        @block.gpsimd
        def _(pool):
            for e in range(2):
                pool.dma_start(raw0[:, e % 2, :], w13[:, e, :, :].rearrange("p a f -> p (a f)"))\
                    .then_inc(w13_slot[e % 2], 16)
            for k, value in enumerate((ATT_EPS, TOK_EPS, ATT_EPS)):
                pool.memset(eps[:, k, :], value).then_inc(setup, 1)
            pool.memset(Qm[:, :, :], 0.0).then_inc(setup, 1)
            pool.memset(cov_acc[:, :], 0.0).then_inc(setup, 1)
            pool.memset(means[:, :], 0.0).then_inc(setup, 1)
            pool.wait_ge(setup, 6)
            pool.wait_ge(ld_const, 32)
            schedule(pool.Fori, pool_span)
            pool.wait_ge(newton, TRACE_STEP)
            pool.tensor_tensor(rstrace[:, :], trace[:, :], con("minus_half")[:, 0:1], ALU.pow).then_inc(wh_ready, 1)
            schedule_1(pool.Fori, pool_span)

        def act_att(n, s):
            act = nc.scalar
            if s == ATT_STEP["T"]:
                after(act, att_full, n * ATT_FILLS + ATT_FILL["T"] + 1)
                act.activation(yaT[:, :], bank[:, ATT0, :], ACT.Copy).then_inc(att_free, 1)
            if s == ATT_STEP["V"]:
                after(act, att_full, n * ATT_FILLS + ATT_FILL["V"] + 1)
                act.activation(Vp[:, :, :].rearrange("p w c -> p (w c)"), bank[:, ATT0, :], ACT.Copy)\
                    .then_inc(att_free, 1)
                after(act, k_r, n + 1)
                for j in range(4):
                    act.activation(Kbd[:, :, j, :], kr.rearrange("p (w m) -> p w m", w=BW), ACT.Copy,
                                   scale=con("in_quad")[:, j:j + 1]).then_inc(k_bd, 1)
            for k in range(BT):
                if s == ATT_STEP[f"T{k}"]:
                    after(act, att_full, n * ATT_FILLS + ATT_FILL[f"T{k}"] + 1)
                    act.activation(PT[:, :, :].rearrange("p a n -> p (a n)"),
                                   bank[:, ATT0:ATT1 + 1, :].rearrange("p b n -> p (b n)"), ACT.Copy)\
                        .then_inc(att_free, 1)
                if s == ATT_STEP[f"O{k}"]:
                    after(act, att_full, n * ATT_FILLS + ATT_FILL[f"O{k}"] + 1)
                    act.activation(On[:, :, k * P:(k + 1) * P].rearrange("p j (w n) -> p w j n", w=2),
                                   bank[:, ATT0, :].rearrange("p (w j n) -> p w j n", w=2, j=4), ACT.Copy)\
                        .then_inc(att_free, 1)
            for k in range(BT):
                if s == EXP_STEP[k]:
                    after(act, att_free, n * ATT_FILLS + ATT_FILL[f"S{k}"] + 1)
                    act.activation(Sx[:, k % 3, :], Sx[:, k % 3, :], ACT.Exp).then_inc(p_exp, 1)

        def act_prep(sp, n, s, layer, p):
            act, at = nc.scalar, PREP_SLOT[layer]
            if layer and s == at["wturn"]:
                after(act, wt_ps, n - BLOCKS + 1)
                act.activation(fts[:, :], bank[:, ATT0, :], ACT.Copy).then_inc(fts_sb, 1)
            if s == at["turn"]:
                after(act, side_full, sp.before("turn") + 1)
                after(act, xl_sb, n)
                act.activation(ymT[:, :], bank[:, SIDE, :], ACT.Copy).then_inc(side_free, 1)
                after(act, side_free, sp.before("turn") + 1)
                after(act, gu_full, n * UNITS - UNITS)
                act.activation(xh[:, p, :], ymT[:, :], ACT.Copy).then_inc(xh_sb, 1)
            if s == at["exp"]:
                after(act, l_sub, n + 1)
                act.activation(lex[:, :, :], lex[:, :, :], ACT.Exp).then_inc(l_exp, 1)
            if s == at["gate_rows"]:
                after(act, side_full, sp.before("gate_rows") + 1)
                gates = bank[0:SPLIT * E, SIDE, 0:BLOCK // 2].bitcast(BF16)
                if layer:
                    act.activation(gTf[:, p, :], gates, ACT.Copy).then_inc(gTf_sb, 1)
                act.activation(gT[:, p, :], gates, ACT.Copy).then_inc(side_free, 1)

        def act_unit(sp, n, u, layer):
            act = nc.scalar
            if layer and sp.first(BLOCKS) and u == 0:
                act.wait_ge(bias_sb, 1)
            after(act, gu_full, n * UNITS + (u + 1))
            after(act, h_sb, n * UNITS + (u - 1))
            bias = gv_bias[:, u:u + 1] if layer else 0.0
            act.activation(silu[:, u % 2, :], G(u), ACT.Silu, bias=bias).then_inc(g_read, 1)
            if u % FT == 0:
                e = u // FT
                after(act, side_full, sp.before(f"C{e}") + 1)
                after(act, h2_sb, n * UNITS + (FT * (e - 1)))
                act.activation(csb[:, e % 2, :], bank[:, SIDE, :], ACT.Copy).then_inc(side_free, 1)

        def act_span(sp):
            for s in range(UNITS):
                if sp.experts:
                    act_unit(sp, sp.n, s, sp.layer)
                if sp.post and s == POST_SLOT - 1:
                    after(nc.scalar, h2_used, sp.n * UNITS)
                    nc.scalar.activation(ob[:, :], bank[:, ACC, :], ACT.Copy).then_inc(ob_sb, 1)
                for n, a in sp.attention(s):
                    act_att(n, a)
                if sp.prep is not None:
                    act_prep(sp, sp.prep, s, sp.layer, sp.p if not sp.experts else 1 - sp.p)
                if sp.setup is not None and 0 <= sp.setup + s < UNITS:
                    act_setup(sp.setup + s)
                if s in sp.folds:
                    act_fold(sp.folds[s])

        def act_setup(s):
            act, e = nc.scalar, s // 2
            if s % 2 == 0:
                act.wait_ge(w13_slot[e % 2], 16 * (e // 2 + 1))
                act.activation(Wh[0][:, e, :], raw0[:, e % 2, :], ACT.Copy).then_inc(w0h, 1)

        def act_fold(e):
            nc.scalar.wait_ge(fold_ps, e + 1)
            nc.scalar.activation(Wh[1][:, e, :], G(e), ACT.Copy).then_inc(w1h, 1)

        @block.scalar
        def _(act):
            act.dma_start(qkv_w[:, :, :], att_w).then_inc(ld_att, 16)
            act.dma_start(S[:, :], small).then_inc(ld_small, 16)
            act.dma_start(wo[:, :, :], proj_w).then_inc(ld_att, 16)
            act.wait_ge(ld_const, 32)
            schedule(act.Fori, act_span)
            for e in range(1, 6):
                act_fold(e)
            schedule_1(act.Fori, act_span)

        def dve_stats(n, s, i):
            dve = nc.vector
            dve.sem_inc(wait_done)
            for k in range(BT):
                nc.vector.bn_stats(stats[s][:, k, :], xt(i, k)).then_inc(ln[s]["stats"], 1)
            after(dve, ln[s]["var"], n)
            for k in range(BT):
                after(dve, ln[s]["stats"], n * BT + k + 1)
                dve.sem_inc(wait_done)
                nc.vector.bn_aggr(mv[s][:, k, :], stats[s][:, k, :]).then_inc(ln[s]["mv"], 1)

        def dve_y(n, s, i, y):
            dve = nc.vector
            after(dve, ln[s]["mv"], n * BT + BT)
            after(dve, ln[s]["rstd"], n + 1)
            for k in range(BT):
                nc.vector.tensor_scalar(y[:, k, :], xt(i, k), mv[s][:, k, 0:1], rstd[s][:, k:k + 1],
                                        ALU.subtract, ALU.mult).then_inc(ln[s]["y"], 1)

        def dve_att(n, s):
            dve = nc.vector
            fills = n * ATT_FILLS
            if s == 0:
                dve_stats(n, "a", n)
            if s == 1:
                after(dve, att_full, fills - ATT_FILLS + 1)
                dve_y(n, "a", n, ya)

            def rotate(dst, half_, col, done):
                table = con("rope")[:, col * WIN:(col + 1) * WIN].unsqueeze(1).to_broadcast([P, BW, WIN])
                nc.vector.scalar_tensor_tensor(
                    out=dst[:, half_, :].rearrange("p (w m) -> p w m", w=BW),
                    in0=bank[:, ATT0 + half_, :].rearrange("p (w m) -> p w m", w=BW),
                    scalar=par("qk_bias")[:, col:col + 1], in1=table, op0=ALU.add, op1=ALU.mult).then_inc(done, 1)

            for fill, dst, done, used, base in (("Q", tq, q_t, q_m, 0), ("K", tk, k_t, k_bd, 2)):
                if s == ATT_STEP[fill]:
                    after(dve, att_full, fills + ATT_FILL[fill] + 1)
                    after(dve, used, n * 4)
                    rotate(dst, 0, base, done)
                    rotate(dst, 1, base + 1, att_free)

            for k in range(BT):
                if s == ATT_STEP[f"S{k}"]:
                    after(dve, att_full, fills + ATT_FILL[f"S{k}"] + 1)
                    sc = bank[:, ATT0:ATT1 + 1, :].rearrange("p b (h m) -> p (b h) m", m=WIN)
                    nc.vector.tensor_reduce(smax[:, k, :], sc, AXIS_X, ALU.max).then_inc(s_max, 1)
                    after(dve, s_max, n * BT + k + 1)
                    nc.vector.tensor_tensor(
                        Sx[:, k % 3, :].rearrange("p (h m) -> p h m", h=HEADS), sc,
                        smax[:, k, :].unsqueeze(2).to_broadcast([P, HEADS, WIN]), ALU.subtract).then_inc(att_free, 1)
            for k, at in enumerate(EXP_STEP):
                if s == at:
                    after(dve, p_exp, n * BT + k + 1)
                    nc.vector.tensor_reduce(ssum[:, k, :], Sx[:, k % 3, :].rearrange("p (h m) -> p h m", h=HEADS),
                                            AXIS_X, ALU.add).then_inc(p_sum, 1)
                    after(dve, p_sum, n * BT + k + 1)
                    nc.vector.reciprocal(srec[:, k, :], ssum[:, k, :]).then_inc(p_rec, 1)
            if s == ATT_STEP["J"]:
                after(dve, x_bias, n + 1)
                after(dve, att_full, fills + ATT_FILL["J"] + 1)
                nc.vector.tensor_tensor(xb(n), xb(n), bank[:, ATT0, :].rearrange("p (t c) -> p t c", t=BT), ALU.add)\
                    .then_inc(att_free, 1)

        def dve_prep(sp, n, s, layer):
            dve, at, i = nc.vector, PREP_SLOT[layer], stream_block(n, layer)
            if layer and s == at["centre"]:
                after(dve, wt_ps, i)
                for k in range(BT):
                    nc.vector.tensor_scalar(yc[:, k, :], xt(i, k), keep[:, bass.ds(i * BT + k, 1), 0],
                                            keep[:, bass.ds(i * BT + k, 1), 1], ALU.subtract, ALU.mult)\
                        .then_inc(wy_sb, 1)
                after(dve, wy_sb, i * BT + BT)
                nc.vector.tensor_tensor(yc[:, :, :], yc[:, :, :], over_tiles(mean_c), ALU.subtract)\
                    .then_inc(wf_sb, 1)
            if layer and s == at["whiten"]:
                after(dve, x_beta, i + 1)
                after(dve, wh_ps, i + 1)
                nc.vector.tensor_tensor(xb(i), xb(i), bank[:, ATT1, :].rearrange("p (t c) -> p t c", t=BT), ALU.add)\
                    .then_inc(x_wh, 1)
            if s == at["ln"]:
                if layer:
                    after(dve, x_wh, i + 1)
                else:
                    after(dve, att_free, n * ATT_FILLS + ATT_FILLS)
                dve_stats(n, "m", i)
            if s == at["y"]:
                after(dve, xh_sb, n)
                dve_y(n, "m", i, ym)
            if s == at["rank"]:
                after(dve, side_full, sp.before("route") + 1)
                logits = bank[:, SIDE, 0:BT * E].rearrange("p (t e) -> p t e", t=BT)
                if layer:
                    ins = nc.vector.tensor_tensor(lg[:, :, :], logits,
                                                  par("router1_bias").unsqueeze(1).to_broadcast([P, BT, E]), ALU.add)
                else:
                    ins = nc.vector.tensor_copy(lg[:, :, :], logits)
                ins.then_inc(side_free, 1)
                after(dve, side_free, sp.before("route") + 1)
                nc.vector.tensor_reduce(lmax[:, :], lg[:, :, :], AXIS_X, ALU.max).then_inc(l_max, 1)
                other = lg[:, :, :].unsqueeze(2).to_broadcast([P, BT, E, E])
                own = lg[:, :, :].unsqueeze(3).to_broadcast([P, BT, E, E])
                nc.vector.tensor_tensor(cmp1[:, :, :, :], other, own, ALU.is_gt).then_inc(l_cmp, 1)
                nc.vector.tensor_tensor(cmp2[:, :, :, :], other, own, ALU.is_equal).then_inc(l_cmp, 1)
                after(dve, l_max, n + 1)
                nc.vector.tensor_tensor(lex[:, :, :], lg[:, :, :], lmax[:, :].unsqueeze(2).to_broadcast([P, BT, E]),
                                        ALU.subtract).then_inc(l_sub, 1)
                after(dve, l_cmp, n * 4 + 2)
                flat = cmp2[:, :, :, :].rearrange("p t e f -> p t (e f)")
                nc.vector.tensor_tensor(flat, flat, con("earlier").unsqueeze(1).to_broadcast([P, BT, E * E]),
                                        ALU.mult).then_inc(l_cmp, 1)
                after(dve, l_cmp, n * 4 + 3)
                nc.vector.tensor_tensor(cmp1[:, :, :, :], cmp1[:, :, :, :], cmp2[:, :, :, :], ALU.add)\
                    .then_inc(l_cmp, 1)
                after(dve, l_cmp, n * 4 + 4)
                nc.vector.tensor_reduce(rank[:, :, :], cmp1[:, :, :, :], AXIS_X, ALU.add).then_inc(l_rank, 1)
            if s == at["gates"]:
                after(dve, l_exp, n + 1)
                if layer:
                    nc.vector.tensor_reduce(gsum[:, :], lex[:, :, :], AXIS_X, ALU.add).then_inc(g_sum, 1)
                after(dve, l_rank, n + 1)
                nc.vector.scalar_tensor_tensor(out=gate[:, :, :], in0=rank[:, :, :], scalar=1.5, in1=lex[:, :, :],
                                               op0=ALU.is_lt, op1=ALU.mult).then_inc(l_sel, 1)
                after(dve, l_sel, n + 1)
                if not layer:
                    nc.vector.tensor_reduce(gsum[:, :], gate[:, :, :], AXIS_X, ALU.add).then_inc(g_sum, 1)
                after(dve, g_sum, n + 1)
                nc.vector.reciprocal(lmax[:, :], gsum[:, :]).then_inc(g_rec, 1)
                after(dve, g_rec, n + 1)
                nc.vector.tensor_tensor(gate[:, :, :], gate[:, :, :], lmax[:, :].unsqueeze(2).to_broadcast([P, BT, E]),
                                        ALU.mult).then_inc(g_sb, 1)
                after(dve, g_sb, n * 6 + 1)
                nc.vector.tensor_copy(g3[:, :, 0, :], gate[:, :, :]).then_inc(g_sb, 1)
                after(dve, g_sb, n * 6 + 2)
                nc.vector.tensor_tensor(gres[:, :, :], gate[:, :, :], g3[:, :, 0, :], ALU.subtract).then_inc(g_sb, 1)
                after(dve, g_sb, n * 6 + 3)
                nc.vector.tensor_copy(g3[:, :, 1, :], gres[:, :, :]).then_inc(g_sb, 1)
                after(dve, g_sb, n * 6 + 4)
                nc.vector.tensor_tensor(gate[:, :, :], gres[:, :, :], g3[:, :, 1, :], ALU.subtract).then_inc(g_sb, 1)
                after(dve, g_sb, n * 6 + 5)
                nc.vector.tensor_copy(g3[:, :, 2, :], gate[:, :, :]).then_inc(g_sb, 1)

        def dve_unit(n, u, layer):
            dve = nc.vector
            after(dve, g_read, n * UNITS + (u + 1))
            after(dve, h2_sb, n * UNITS + (u - 1))
            if layer:
                ins = nc.vector.scalar_tensor_tensor(
                    out=h[:, u % 2, :], in0=U(u), scalar=gv_bias[:, UNITS + u:UNITS + u + 1],
                    in1=silu[:, u % 2, :], op0=ALU.add, op1=ALU.mult)
            else:
                ins = nc.vector.tensor_tensor(h[:, u % 2, :], silu[:, u % 2, :], U(u), ALU.mult)
            ins.then_inc(h_sb, 1)

        def dve_cov(sp, n, s):
            dve = nc.vector
            if s == COV_SLOT["ln"]:
                after(dve, x_moe, n + 1)
                dve_stats(n, "c", n)
            if s == COV_SLOT["y"]:
                dve_y(n, "c", n, yc)
                nc.vector.tensor_copy(keep[:, bass.ds(n * BT, BT), 0], mv["c"][:, :, 0]).then_inc(kept, 1)
                nc.vector.tensor_copy(keep[:, bass.ds(n * BT, BT), 1], rstd["c"][:, :]).then_inc(kept, 1)
            if s == COV_SLOT["mean"]:
                after(dve, side_full, sp.before("mean") + 1)
                nc.vector.scalar_tensor_tensor(out=means[:, :], in0=bank[:, SIDE, 0:P], scalar=ident[:, bass.ds(n, 1)],
                                               in1=means[:, :], op0=ALU.mult, op1=ALU.add).then_inc(mean_row, 1)
                after(dve, mean_row, n + 1)
                nc.vector.tensor_tensor(yc[:, :, :], yc[:, :, :], over_tiles(bank[:, SIDE, 0:P]), ALU.subtract)\
                    .then_inc(side_free, 1)
            if s == COV_SLOT["cov"]:
                after(dve, side_full, sp.before("cov") + 1)
                nc.vector.tensor_tensor(cov_acc[:, :], cov_acc[:, :], bank[:, SIDE, 0:P], ALU.add).then_inc(side_free, 1)

        def dve_span(sp):
            dve = nc.vector
            for s in range(UNITS):
                if sp.experts:
                    dve_unit(sp.n, s, sp.layer)
                if sp.post and s == POST_SLOT:
                    i = stream_block(sp.n, sp.layer) - 1
                    after(dve, side_full, sp.before("post") + 1)
                    nc.vector.tensor_tensor(xb(i), xb(i), bank[:, SIDE, :].rearrange("p (t c) -> p t c", t=BT), ALU.add)\
                        .then_inc(side_free, 1)
                    after(dve, side_free, sp.before("post") + 1)
                    dve.sem_inc(x_moe)
                if sp.cov:
                    dve_cov(sp, sp.n - 1, s)
                for n, a in sp.attention(s):
                    if sp.first(0) and isinstance(n, int):
                        if n == 0 and a == 1:
                            dve.wait_ge(ld_small, 16)
                            dve.wait_ge(ld_const, 32)
                        if n == 0 and a == 2:
                            dve.wait_ge(abias_ps, 1)
                            nc.vector.tensor_tensor(att_bias[:, :], bank[:, ATT1, 0:P], par("proj_bias"), ALU.add)\
                                .then_inc(abias_sb, 1)
                        if n == 1 and a == 0:
                            dve.wait_ge(ld_x1, 16)
                    dve_att(n, a)
                if sp.prep is not None:
                    dve_prep(sp, sp.prep, s, sp.layer)
                if sp.setup is not None and 0 <= sp.setup + s < UNITS:
                    dve_setup(sp.setup + s)
                if s - 2 in sp.folds:
                    dve_fold(sp.folds[s - 2])

        def dve_setup(s):
            dve, e = nc.vector, s // 2
            if s % 2 == 0:
                dve.wait_ge(w0h, e + 1)
                nc.vector.tensor_tensor(Wl[0][:, e, :], raw0[:, e % 2, :], Wh[0][:, e, :].bitcast(F32), ALU.subtract)\
                    .then_inc(w0l, 1)

        def dve_fold(e):
            dve = nc.vector
            dve.wait_ge(w1h, e + 1)
            nc.vector.tensor_tensor(Wl[1][:, e, :], G(e), Wh[1][:, e, :].bitcast(F32), ALU.subtract).then_inc(w1l, 1)
            if e == E - 1:
                dve.wait_ge(bias_ps, E)
                nc.vector.tensor_tensor(gv_bias[:, :], bank[:, ACC, 0:2 * UNITS], par("gv_bias"), ALU.add)\
                    .then_inc(bias_sb, 1)

        @block.vector
        def _(dve):
            dve.wait_ge(setup, 6)
            dve.wait_ge(ld_x0, 16)
            schedule(dve.Fori, dve_span)
            step = [0]

            def link(ins):
                ins.then_inc(newton, 1)
                step[0] += 1
                dve.wait_ge(newton, step[0])

            dve.wait_ge(newton_ps, 1)
            link(nc.vector.tensor_scalar(mean_c, bank[:, ATT0, 0:P], float(BLOCK // BLOCKS), None, ALU.mult))
            link(nc.vector.tensor_tensor(means[0:BLOCKS, :], means[0:BLOCKS, :], mean_c[0:BLOCKS, :], ALU.subtract))
            dve_fold(1)
            dve.wait_ge(newton_ps, 2)
            link(nc.vector.scalar_tensor_tensor(out=cov, in0=bank[:, ATT1, 0:P], scalar=float(BLOCK),
                                                in1=cov_acc[:, :], op0=ALU.mult, op1=ALU.add))
            link(nc.vector.scalar_tensor_tensor(out=cov, in0=cov,
                                                scalar=(1.0 - WHITEN_EPS) / (TOKENS - 1.0), in1=con("same_group"),
                                                op0=ALU.mult, op1=ALU.mult))
            link(nc.vector.scalar_tensor_tensor(out=cov, in0=ident, scalar=WHITEN_EPS, in1=cov,
                                                op0=ALU.mult, op1=ALU.add))
            nc.vector.tensor_tensor(covd, cov, ident, ALU.mult).then_inc(centre_d, 1)
            dve.wait_ge(centre_d, 1)
            link(nc.vector.tensor_reduce(diag[:, :], covd, AXIS_X, ALU.add))
            dve.wait_ge(newton_ps, 3)
            link(nc.vector.tensor_copy(trace[:, :], bank[:, ATT0, 0:1]))
            assert step[0] == TRACE_STEP
            link(nc.vector.reciprocal(rtrace[:, :], trace[:, :]))
            link(nc.vector.tensor_scalar(sig, cov, rtrace[:, 0:1], None, ALU.mult))
            link(nc.vector.tensor_scalar(tmpn, sig, -0.5, None, ALU.mult))
            link(nc.vector.scalar_tensor_tensor(out=Pm[:, 0, :], in0=ident, scalar=1.5, in1=tmpn,
                                                op0=ALU.mult, op1=ALU.add))
            assert step[0] == FIRST_STEP
            dve_fold(2)
            for it in range(NEWTON_STEPS - 1):
                old, new = Pm[:, it % 2, :], Pm[:, (it + 1) % 2, :]
                dve.wait_ge(newton_ps, 3 * it + 4)
                link(nc.vector.tensor_copy(N1, bank[:, ATT0, 0:P]))
                dve.wait_ge(newton_ps, 3 * it + 5)
                link(nc.vector.tensor_copy(N2, bank[:, ATT1, 0:P]))
                if it:
                    dve_fold(4)
                dve.wait_ge(newton_ps, 3 * it + 6)
                link(nc.vector.tensor_scalar(tmpn, bank[:, ATT0, 0:P], -0.5, None, ALU.mult))
                link(nc.vector.scalar_tensor_tensor(out=new, in0=old, scalar=1.5, in1=tmpn,
                                                    op0=ALU.mult, op1=ALU.add))
                dve_fold(3 + 2 * it)
            dve.wait_ge(wh_ready, 1)
            nc.vector.scalar_tensor_tensor(out=whiten, in0=Pm[:, (NEWTON_STEPS - 1) % 2, :],
                                           scalar=rstrace[:, 0:1], in1=par("gamma"), op0=ALU.mult, op1=ALU.mult)\
                .then_inc(wh_ready, 1)
            schedule_1(dve.Fori, dve_span)

        def pe_att(n, s, late):
            pe, mm = nc.tensor, nc.tensor.matmul

            def fill(name):
                after(pe, att_free, n * ATT_FILLS + ATT_FILL[name])

            def at(name):
                return s == ATT_STEP[name] and late == (name in ATT_LATE)

            if at("T"):
                fill("T")
                after(pe, ln["a"]["y"], n * BT + BT)
                for k in range(BT):
                    last = nc.tensor.transpose(bank[:, ATT0, k * P:(k + 1) * P], ya[:, k, :], ident)
                last.then_inc(att_full, 1)
            if at("Q") and isinstance(n, int) and n == 0:
                pe.wait_ge(abias_sb, 1)
            for name, w in (("Q", 0), ("K", 2)):
                if at(name):
                    fill(name)
                    mm(bank[:, ATT0, :], qkv_w[:, w, :], yaT[:, :], start=True, stop=True)
                    mm(bank[:, ATT1, :], qkv_w[:, w + 1, :], yaT[:, :], start=True, stop=True)\
                        .then_inc(att_full, 1)
            if at("V"):
                fill("V")
                for w in range(BW):
                    for hh in range(2):
                        c = slice(64 * hh, 64 * hh + 64)
                        last = mm(bank[c, ATT0, w * WIN:(w + 1) * WIN], yaT[:, w * WIN:(w + 1) * WIN],
                                  qkv_w[:, 4, c], start=True, stop=True)
                last.then_inc(att_full, 1)

            def scores(k):
                fill(f"S{k}")
                if k == 0:
                    after(pe, q_m, n * 4 + 4)
                    after(pe, k_bd, n * 4 + 4)
                for g in range(4):
                    for w in range(2):
                        t = (2 * k + w) * WIN
                        last = mm(bank[w * WIN:(w + 1) * WIN, ATT0 + g // 2, (g % 2) * 256:(g % 2 + 1) * 256],
                                  Qm[:, g, t:t + WIN], Kbd[:, 2 * k + w, :, :].rearrange("p j m -> p (j m)"),
                                  start=True, stop=True)
                last.then_inc(att_full, 1)

            def turned(k):
                fill(f"T{k}")
                after(pe, p_nrm, n * BT + k + 1)
                for a in range(HP):
                    last = nc.tensor.transpose(bank[:, ATT0 + a // 4, (a % 4) * P:(a % 4 + 1) * P],
                                               Sx[:, k % 3, a * P:(a + 1) * P], ident)
                last.then_inc(att_full, 1)

            def values(k):
                fill(f"O{k}")
                pe.sem_inc(wait_done)
                for w in range(2):
                    for q in range(2):
                        for hh in range(2):
                            r, o = slice(64 * hh, 64 * hh + 64), 32 * (2 * hh + q)
                            last = mm(bank[o:o + 32, ATT0, w * 256:(w + 1) * 256],
                                      Vp[r, 2 * k + w, q * 32:(q + 1) * 32],
                                      PT[r, 4 * q:4 * q + 4, w * WIN:(w + 1) * WIN], start=True, stop=True)
                last.then_inc(att_full, 1)

            for k in range(BT):
                if at(f"T{k}"):
                    turned(k)
                if at(f"O{k}"):
                    values(k)
            for k in range(BT):
                if at(f"S{k}"):
                    scores(k)
            if at("J"):
                fill("J")
                for k in range(BT):
                    for j in range(4):
                        last = mm(bank[:, ATT0, k * P:(k + 1) * P], On[:, j, k * P:(k + 1) * P], wo[:, j, :],
                                  start=(j == 0), stop=(j == 3))
                last.then_inc(att_full, 1)

        def pe_prep(sp, n, s, layer, p):
            pe, mm, at = nc.tensor, nc.tensor.matmul, PREP_SLOT[layer]
            if layer and s == at["wturn"]:
                i = n - BLOCKS
                after(pe, wf_sb, i + 1)
                after(pe, fts_sb, i)
                for k in range(BT):
                    last = nc.tensor.transpose(bank[:, ATT0, k * P:(k + 1) * P], yc[:, k, :], ident)
                last.then_inc(wt_ps, 1)
            if layer and s == at["whiten"]:
                i = n - BLOCKS
                after(pe, fts_sb, i + 1)
                after(pe, x_wh, i)
                for k in range(BT):
                    last = mm(bank[:, ATT1, k * P:(k + 1) * P], fts[:, k * P:(k + 1) * P], whiten,
                              start=True, stop=True)
                last.then_inc(wh_ps, 1)
            if s == at["turn"]:
                after(pe, side_free, sp.before("turn"))
                after(pe, ln["m"]["y"], n * BT + BT)
                for k in range(BT):
                    last = nc.tensor.transpose(bank[:, SIDE, k * P:(k + 1) * P], ym[:, k, :], ident)
                last.then_inc(side_full, 1)
            if s == at["route"]:
                after(pe, side_free, sp.before("route"))
                after(pe, xh_sb, n + 1)
                for k in range(BT):
                    last = mm(bank[:, SIDE, k * E:(k + 1) * E], ymT[:, k * P:(k + 1) * P],
                              par(f"router{layer}"), start=True, stop=True)
                last.then_inc(side_full, 1)
            if s == at["gate_rows"]:
                after(pe, side_free, sp.before("gate_rows"))
                after(pe, g_sb, n * 6 + 6)
                gates = bank[0:SPLIT * E, SIDE, 0:BLOCK // 2].bitcast(BF16)
                for k in range(BT):
                    last = nc.tensor.transpose(gates[:, k * P:(k + 1) * P],
                                               g3[:, k, :, :].rearrange("p s e -> p (s e)"), ident_b)
                last.then_inc(side_full, 1)

        def pe_up(sp, n, u, layer, p):
            pe, mm = nc.tensor, nc.tensor.matmul
            e, ft = u // FT, u % FT
            if u == 0:
                after(pe, xl_sb, n + 1)
            after(pe, h_sb, n * UNITS + (u - 1))
            for part, dst in ((0, G(u)), (1, U(u))):
                c = part * FF + ft * P
                wh, wl = Wh[layer][:, e, c:c + P], Wl[layer][:, e, c:c + P]
                mm(dst, wh, xh[:, p, :], start=True, stop=False)
                mm(dst, wh, xl[:, p, :], start=False, stop=False)
                last = mm(dst, wl, xh[:, p, :], start=False, stop=True)
            last.then_inc(gu_full, 1)
            if ft == 0:
                after(pe, side_free, sp.before(f"C{e}"))
                mm(bank[:, SIDE, :], select[:, e, :], gT[:, p, :], start=True, stop=True).then_inc(side_full, 1)

        def pe_down(n, u, layer, p):
            pe, mm = nc.tensor, nc.tensor.matmul
            after(pe, h2_sb, n * UNITS + (u + 1))
            if u == 0:
                after(pe, ob_sb, n)
                if layer:
                    after(pe, gTf_sb, n - (BLOCKS - 1))
                    mm(bank[:, ACC, :], par("b2")[0:SPLIT * E, :], gTf[:, p, :], start=True, stop=False)
            mm(bank[:, ACC, :], W2[layer][:, u, :], h2[:, u % 4, :],
               start=(u == 0 and not layer), stop=(u == UNITS - 1)).then_inc(h2_used, 1)

        def pe_span(sp):
            pe, mm = nc.tensor, nc.tensor.matmul
            if sp.experts and sp.first(0):
                pe.wait_ge(ld_w2, 32)
                pe.wait_ge(w0h, E)
                pe.wait_ge(w0l, E)
            if sp.experts and sp.first(BLOCKS):
                pe.wait_ge(w1l, E)
                pe.wait_ge(bias_sb, 1)
            for s in range(UNITS):
                if sp.experts:
                    pe_up(sp, sp.n, s, sp.layer, sp.p)
                for n, a in sp.attention(s):
                    pe_att(n, a, False)
                if sp.experts and s >= DOWN_LAG:
                    pe_down(sp.n, s - DOWN_LAG, sp.layer, sp.p)
                elif sp.post and s < DOWN_LAG:
                    pe_down(sp.n - 1, UNITS + s - DOWN_LAG, sp.layer, 1 - sp.p)
                if sp.post and s == POST_SLOT:
                    after(pe, side_free, sp.before("post"))
                    after(pe, ob_sb, sp.n)
                    for k in range(BT):
                        last = nc.tensor.transpose(bank[:, SIDE, k * P:(k + 1) * P], ob[:, k * P:(k + 1) * P], ident)
                    last.then_inc(side_full, 1)
                if sp.cov and s == COV_SLOT["mean"]:
                    after(pe, side_free, sp.before("mean"))
                    after(pe, ln["c"]["y"], sp.n * BT)
                    for k in range(BT):
                        last = mm(bank[:, SIDE, 0:P], con("block_mean"), yc[:, k, :], start=(k == 0),
                                  stop=(k == BT - 1))
                    last.then_inc(side_full, 1)
                if sp.cov and s == COV_SLOT["cov"]:
                    after(pe, side_free, sp.before("cov"))
                    for k in range(BT):
                        last = mm(bank[:, SIDE, 0:P], yc[:, k, :], yc[:, k, :], start=(k == 0), stop=(k == BT - 1))
                    last.then_inc(side_full, 1)
                if sp.prep is not None:
                    pe_prep(sp, sp.prep, s, sp.layer, sp.p if not sp.experts else 1 - sp.p)
                for n, a in sp.attention(s):
                    pe_att(n, a, True)
                if s in sp.folds:
                    pe_fold(sp.folds[s])
                    pe_fold_bias(sp.folds[s])

        def pe_fold(e):
            pe, mm = nc.tensor, nc.tensor.matmul
            pe.wait_ge(w1gv_slot[e % RAW_SLOTS], 16 * (e // RAW_SLOTS + 1))
            if e >= 2:
                pe.wait_ge(w1l, e - 1)
            else:
                after(pe, h_sb, BLOCKS * UNITS)
            raw = raw1[:, e % RAW_SLOTS, :]
            for ht in range(FT):
                last = mm(G(e), raw[:, ht * P:(ht + 1) * P], raw[:, FF + ht * 2 * FF:FF + (ht + 1) * 2 * FF],
                          start=(ht == 0), stop=(ht == FT - 1))
            last.then_inc(fold_ps, 1)

        def pe_fold_bias(e):
            pe, mm = nc.tensor, nc.tensor.matmul
            raw = raw1[:, e % RAW_SLOTS, :]
            if e == 0:
                after(pe, ob_sb, BLOCKS)
            for part in range(2):
                for ft in range(FT):
                    col = part * UNITS + e * FT + ft
                    for ht in range(FT):
                        c = FF + ht * 2 * FF + part * FF + ft * P
                        last = mm(bank[:, ACC, col:col + 1], raw[:, c:c + P],
                                  par("b1")[:, e * FT + ht:e * FT + ht + 1], start=(ht == 0), stop=(ht == FT - 1))
            last.then_inc(bias_ps, 1)

        @block.tensor
        def _(pe):
            mm = nc.tensor.matmul
            pe.wait_ge(ld_small, 16)
            pe.wait_ge(ld_att, 32)
            mm(bank[:, ATT1, 0:P], par("v_bias"), wo[:, 4, :], start=True, stop=True).then_inc(abias_ps, 1)
            pe.wait_ge(setup, 6)
            pe.wait_ge(ld_const, 32)
            schedule(pe.Fori, pe_span)
            pe_fold(1)
            pe.wait_ge(mean_row, START + BLOCKS)
            mm(bank[:, ATT0, 0:P], con("block_mean"), means[:, :], start=True, stop=True).then_inc(newton_ps, 1)
            pe_fold_bias(1)
            pe.wait_ge(newton, 2)
            mm(bank[:, ATT1, 0:P], means[0:BLOCKS, :], means[0:BLOCKS, :], start=True, stop=True).then_inc(newton_ps, 1)
            pe_fold(2)
            pe.wait_ge(newton, TRACE_STEP - 1)
            mm(bank[:, ATT0, 0:1], con("same_group"), diag[:, :], start=True, stop=True).then_inc(newton_ps, 1)
            pe_fold_bias(2)
            for it in range(NEWTON_STEPS - 1):
                old = Pm[:, it % 2, :]
                e = 3 + it
                pe.wait_ge(newton, FIRST_STEP + 4 * it)
                mm(bank[:, ATT0, 0:P], old, old, start=True, stop=True).then_inc(newton_ps, 1)
                pe_fold(e) if it == 0 else pe_fold_bias(4)
                pe.wait_ge(newton, FIRST_STEP + 1 + 4 * it)
                mm(bank[:, ATT1, 0:P], N1, old, start=True, stop=True).then_inc(newton_ps, 1)
                pe_fold_bias(e) if it == 0 else pe_fold(5)
                pe.wait_ge(newton, FIRST_STEP + 2 + 4 * it)
                mm(bank[:, ATT0, 0:P], N2, sig, start=True, stop=True).then_inc(newton_ps, 1)
                pe_fold(4) if it == 0 else pe_fold_bias(5)
            pe.wait_ge(wh_ready, 2)
            schedule_1(pe.Fori, pe_span)


def _tokens(x):
    return x.reshape(8, 8, 2, 2, 8, 2, P).transpose(5, 1, 4, 0, 3, 2, 6).reshape(P, TILES, P)


def _image(y):
    return y.reshape(2, 8, 8, 8, 2, 2, P).transpose(3, 1, 5, 4, 2, 0, 6).reshape(4, 32, 32, P)


def _columns(width, at, **arrays):
    table = np.zeros((P, width), np.float32)
    for name, a in arrays.items():
        col, w = at[name]
        table[:a.shape[0], col:col + w] = a
    return table


def _layout(i):
    ch = np.arange(P)
    swapped = ch ^ 1
    by_parity = np.array([(2 * hp + hh) * HD + d for hh in range(2) for hp in range(HP) for d in range(HD)])
    qw, kw, vw = i["L0_conv_qkv_w"].reshape(3, P, P)
    qb, kb, vb = i["L0_conv_qkv_b"].reshape(3, P)
    att_w = np.stack([qw.T, qw[swapped].T, kw.T, kw[swapped].T, vw[by_parity].T], 1)
    pw = i["L0_conv_proj_w"][:, by_parity].T
    place = (ch // HD) % 4
    masked = [np.where((place == j)[:, None], pw, np.float32(0)) for j in range(4)]
    proj_w = np.stack(masked + [pw], 1)
    row = lambda a: np.broadcast_to(a.reshape(1, -1), (P, a.size))
    cols = lambda a: a.reshape(E * FT, P).T
    small = _columns(
        SMALL_WIDTH, SMALL_AT,
        qk_bias=np.stack([qb, qb[swapped], kb, kb[swapped]], 1),
        v_bias=np.broadcast_to(vb[by_parity][:, None], (P, P)),
        proj_bias=row(i["L0_conv_proj_b"]),
        router0=i["L0_ffn_router_w"], router1=i["L1_ffn_router_w"], router1_bias=row(i["L1_ffn_router_b"]),
        gamma=row(i["L1_conv_gamma"]), beta=row(i["L1_conv_beta"]),
        b1=cols(i["L1_ffn_b1"]), gv_bias=np.concatenate([cols(i["L1_ffn_bg"]), cols(i["L1_ffn_bv"])], 1),
        b2=np.concatenate([i["L1_ffn_b2"]] * SPLIT, 0))
    w13 = np.stack([i["L0_ffn_w1"], i["L0_ffn_w3"]], 1).transpose(2, 0, 1, 3)
    down = lambda w: w.reshape(E * FT, P, P).transpose(1, 0, 2)
    w1T = i["L1_ffn_w1"].reshape(E, P, FT, P).transpose(0, 3, 2, 1).reshape(E, P, FT * P)
    gv = np.concatenate([i["L1_ffn_wg"], i["L1_ffn_wv"]], 2).reshape(E, FT, P, 2 * FF).transpose(0, 2, 1, 3)
    return {
        "x": _tokens(i["x"]),
        "const": _columns(CONST_WIDTH, CONST_AT, **constants()),
        "halves": half_constants(),
        "small": small, "att_w": att_w, "proj_w": proj_w, "w13": w13, "w2_0": down(i["L0_ffn_w2"]),
        "w1gv": np.concatenate([w1T, gv.reshape(E, P, FT * 2 * FF)], 2), "w2_1": down(i["L1_ffn_w2"]),
    }


def kernel(**inputs):
    import concourse.bacc as bacc
    from concourse.bass_utils import run_bass_kernel_spmd

    arrays = {k: np.ascontiguousarray(v) for k, v in _layout({k: np.asarray(v) for k, v in inputs.items()}).items()}
    nc = bacc.Bacc("TRN2", target_bir_lowering=False, num_devices=1)
    aps = {k: nc.dram_tensor(f"{k}_dram", v.shape, mybir.dt.from_np(v.dtype), kind="ExternalInput").ap() for k, v in arrays.items()}
    out = nc.dram_tensor("out_dram", (P, TILES, P), F32, kind="ExternalOutput").ap()
    build(nc, out=out, **aps)
    r = run_bass_kernel_spmd(nc, [{f"{k}_dram": v for k, v in arrays.items()}], core_ids=[0])
    return _image(r.results[0]["out_dram"])
```
